# Optimizing a Trainium2 kernel written in Bass

```python
import numpy as np
import jax
import jax.numpy as jnp

def _softmax(x, axis=-1):
    return jax.nn.softmax(x, axis=axis)

def _gelu(x):
    return jax.nn.gelu(x, approximate=True)

def _silu(x):
    return jax.nn.silu(x)

def _sigmoid(x):
    return jax.nn.sigmoid(x)

def _layernorm(x, axis=-1, eps=1e-05):
    m = jnp.mean(x, axis=axis, keepdims=True)
    v = jnp.var(x, axis=axis, keepdims=True)
    return (x - m) / jnp.sqrt(v + eps)

def _scatter_add(tgt, idx, src, axis=0):
    return tgt.at[idx].add(src)

def _segment_sum(src, seg, n):
    return jax.ops.segment_sum(src, seg, n)
kernel_name = 'mk_adj_resnorm_d2_adj_r2_de5d5e'

def setup_inputs(seed: int=0):
    np.random.seed(seed)
    _w = jnp.asarray

    def _rec_inputs():
        import jax
        import jax.numpy as jnp
        _gk = jax.random.key(seed)
        x = -0.000929 + 1 * jax.random.normal(jax.random.fold_in(_gk, 1), (128, 128, 256), jnp.float32)
        _a = jax.random.bernoulli(jax.random.fold_in(_gk, 2), 0.03125, (128, 128))
        adj = _a.astype(jnp.int32)
        return (x, adj)
    x, adj = _rec_inputs()

    def _L0_gnn_setup():
        import jax, jax.numpy as jnp
        import numpy as np
        B, K, DIN, DOUT = (32, 64, 256, 256)
        key = jax.random.key(seed)
        k1, k2, k3, k4 = jax.random.split(key, 4)
        x = jax.random.normal(k1, (B, K, DIN), dtype=jnp.float32)
        adj = jax.random.randint(k2, (K, K), 0, 2, dtype=jnp.int32)
        W = jax.random.normal(k3, (DOUT, 2 * DIN), dtype=jnp.float32) * 0.02
        b = jax.random.normal(k4, (DOUT,), dtype=jnp.float32) * 0.02
        return {'x': x, 'adj': adj, 'W': W, 'b': b}
    _L0_gnn_all = _L0_gnn_setup()
    _L0_gnn_in = {k: v for k, v in _L0_gnn_all.items() if k in ('W', 'b')}
    del _L0_gnn_all

    def _L1_gnn_setup():
        import jax, jax.numpy as jnp
        import numpy as np
        LEAKY_ALPHA = 0.01
        NEG_INF = -1000000000.0
        LN_EPS = 1e-05

        def _gat_heads(x, adj, W, a):
            O = W.shape[-1]
            Wh = jnp.einsum('bnf,hfo->bhno', x, W)
            f1 = jnp.einsum('bhno,ho->bhn', Wh, a[:, :O])
            f2 = jnp.einsum('bhno,ho->bhn', Wh, a[:, O:])
            e = f1[:, :, :, None] + f2[:, :, None, :]
            e = jnp.where(e > 0, e, LEAKY_ALPHA * e)
            e = jnp.where(adj[None, None] > 0, e, NEG_INF)
            attn = jax.nn.softmax(e, axis=-1)
            return jnp.einsum('bhnm,bhmo->bhno', attn, Wh)
        key = jax.random.key(seed)
        ks = jax.random.split(key, 10)
        B, N, F_in, F_hid, H, F_out, D_ff = (8, 1024, 256, 256, 4, 256, 256)
        s = 0.05
        return {'enc_inputs': jax.random.normal(ks[0], (B, N, F_in), jnp.float32), 'adj': jax.random.randint(ks[1], (N, N), 0, 2, jnp.int32), 'W_heads': jax.random.normal(ks[2], (H, F_in, F_hid), jnp.float32) * s, 'a_heads': jax.random.normal(ks[3], (H, 2 * F_hid), jnp.float32) * s, 'W_out': jax.random.normal(ks[4], (H * F_hid, F_out), jnp.float32) * s, 'a_out': jax.random.normal(ks[5], (2 * F_out,), jnp.float32) * s, 'w1': jax.random.normal(ks[6], (F_out, D_ff), jnp.float32) * s, 'b1': jnp.zeros((D_ff,), jnp.float32), 'w2': jax.random.normal(ks[7], (D_ff, F_out), jnp.float32) * s, 'b2': jnp.zeros((F_out,), jnp.float32), 'ln_gamma': jnp.ones((F_out,), jnp.float32), 'ln_beta': jnp.zeros((F_out,), jnp.float32)}
    _L1_gnn_all = _L1_gnn_setup()
    _L1_gnn_in = {k: v for k, v in _L1_gnn_all.items() if k in ('W_heads', 'a_heads', 'W_out', 'a_out', 'w1', 'b1', 'w2', 'b2', 'ln_gamma', 'ln_beta')}
    del _L1_gnn_all
    return {'x': x, 'adj': adj, 'L0_gnn_W': _L0_gnn_in['W'], 'L0_gnn_b': _L0_gnn_in['b'], 'L1_gnn_W_heads': _L1_gnn_in['W_heads'], 'L1_gnn_a_heads': _L1_gnn_in['a_heads'], 'L1_gnn_W_out': _L1_gnn_in['W_out'], 'L1_gnn_a_out': _L1_gnn_in['a_out'], 'L1_gnn_w1': _L1_gnn_in['w1'], 'L1_gnn_b1': _L1_gnn_in['b1'], 'L1_gnn_w2': _L1_gnn_in['w2'], 'L1_gnn_b2': _L1_gnn_in['b2'], 'L1_gnn_ln_gamma': _L1_gnn_in['ln_gamma'], 'L1_gnn_ln_beta': _L1_gnn_in['ln_beta']}

def reference(x, adj, L0_gnn_W, L0_gnn_b, L1_gnn_W_heads, L1_gnn_a_heads, L1_gnn_W_out, L1_gnn_a_out, L1_gnn_w1, L1_gnn_b1, L1_gnn_w2, L1_gnn_b2, L1_gnn_ln_gamma, L1_gnn_ln_beta):
    import jax
    import jax.numpy as jnp

    def _L0_gnn_ref(x, adj, W, b):
        import jax, jax.numpy as jnp
        import numpy as np
        B, K, DIN, DOUT = (32, 64, 256, 256)
        Din = x.shape[-1]
        Wi, Wj = (W[:, :Din], W[:, Din:])
        mi = jnp.einsum('bkd,od->bko', x, Wi)
        mj = jnp.einsum('bkd,od->bko', x, Wj)
        a = adj.astype(x.dtype)
        deg = a.sum(axis=1)
        out = deg[None, :, None] * (mi + b) + jnp.einsum('ij,bjo->bio', a, mj)
        return out

    def _L1_gnn_ref(enc_inputs, adj, W_heads, a_heads, W_out, a_out, w1, b1, w2, b2, ln_gamma, ln_beta):
        import jax, jax.numpy as jnp
        import numpy as np
        LEAKY_ALPHA = 0.01
        NEG_INF = -1000000000.0
        LN_EPS = 1e-05

        def _gat_heads(x, adj, W, a):
            O = W.shape[-1]
            Wh = jnp.einsum('bnf,hfo->bhno', x, W)
            f1 = jnp.einsum('bhno,ho->bhn', Wh, a[:, :O])
            f2 = jnp.einsum('bhno,ho->bhn', Wh, a[:, O:])
            e = f1[:, :, :, None] + f2[:, :, None, :]
            e = jnp.where(e > 0, e, LEAKY_ALPHA * e)
            e = jnp.where(adj[None, None] > 0, e, NEG_INF)
            attn = jax.nn.softmax(e, axis=-1)
            return jnp.einsum('bhnm,bhmo->bhno', attn, Wh)
        B, N, _ = enc_inputs.shape
        h = jax.nn.elu(_gat_heads(enc_inputs, adj, W_heads, a_heads))
        h = jnp.transpose(h, (0, 2, 1, 3)).reshape(B, N, -1)
        out = _gat_heads(h, adj, W_out[None], a_out[None])[:, 0]
        out = jax.nn.elu(out)
        ffn = jnp.maximum(out @ w1 + b1, 0.0) @ w2 + b2
        y = ffn + out
        mu = jnp.mean(y, axis=-1, keepdims=True)
        var = jnp.var(y, axis=-1, keepdims=True)
        return (y - mu) / jnp.sqrt(var + LN_EPS) * ln_gamma + ln_beta
    x = _layernorm(x + _L0_gnn_ref(x, adj, L0_gnn_W, L0_gnn_b), axis=-1)
    x = _layernorm(x + _L1_gnn_ref(x, adj, L1_gnn_W_heads, L1_gnn_a_heads, L1_gnn_W_out, L1_gnn_a_out, L1_gnn_w1, L1_gnn_b1, L1_gnn_w2, L1_gnn_b2, L1_gnn_ln_gamma, L1_gnn_ln_beta), axis=-1)
    return x

_drawn_inputs = setup_inputs


def setup_inputs(seed=0):
    import zlib

    import numpy as np

    out = dict(_drawn_inputs(seed))
    spreads = {'L1_gnn_b1': (0.0, 0.1),
     'L1_gnn_b2': (0.0, 0.1),
     'L1_gnn_ln_gamma': (1.0, 0.2),
     'L1_gnn_ln_beta': (0.0, 0.1)}
    factors = {}
    for name, (base, spread) in spreads.items():
        noise = np.random.default_rng([zlib.crc32(name.encode()), seed]).standard_normal(out[name].shape)
        drawn = base * np.exp(spread * noise) if base else spread * noise
        out[name] = jnp.asarray(drawn.astype(out[name].dtype))
    for name, factor in factors.items():
        out[name] = (out[name] * factor).astype(out[name].dtype)
    return out
```

```python
from contextlib import ExitStack

import concourse.bass as bass
from concourse import mybir

ALU = mybir.AluOpType
ACT = mybir.ActivationFunctionType
F32 = mybir.dt.float32
F32R = mybir.dt.float32r
BF16 = mybir.dt.bfloat16
I32 = mybir.dt.int32
AX_X = mybir.AxisListType.X

P = 128
UNROLL = 4
LAST_STAGE = 4
REACH = 6
AHEAD = 3
MASKED = -float(2**100)
EPS = 1e-5
SLOPE = 0.01


class Pair:

    def __init__(self, turn, off, pairs):
        self.turn, self.off, self.pairs = turn, off, pairs

    def back(self, k):
        return Pair(self.turn, self.off - k, self.pairs)

    def there(self):
        return not isinstance(self.turn, int) or 0 <= self.off < self.pairs

    def slot(self, n):
        return self.off % n

    def index(self):
        return self.turn * UNROLL + self.off

    def count(self, per, k):
        return self.turn * (UNROLL * per) + (self.off * per + k)


def after(eng, sem, pair, per=1, k=None):
    if pair.there():
        eng.wait_ge(sem, pair.count(per, per if k is None else k))


def over_steps(eng, pairs, step):
    full = (pairs - REACH - AHEAD) // UNROLL
    for t in range(REACH):
        step(Pair(0, t, pairs))
    with eng.Fori(0, full) as turn:
        for j in range(UNROLL):
            step(Pair(turn, REACH + j, pairs))
    for t in range(REACH + UNROLL * full, pairs + LAST_STAGE):
        step(Pair(0, t, pairs))


def graph_layers(nc, x, adj, adj_t, w0_t, b0, w_heads, a_heads, w_out, a_out, w1, b1, w2, b2, gamma, beta, out):
    graphs, N, F = x.shape
    H = a_heads.shape[0]
    C = F // P
    PAIRS = graphs // 2
    HC = H * C
    assert N == P and F == 2 * P and H == 4 and graphs % 2 == 0

    x_pairs = x.rearrange("(p b) n f -> p n b f", b=2)
    out_pairs = out.rearrange("(p b) n f -> p n b f", b=2)

    with ExitStack() as ctx:
        def sb(name, shape, dt=F32):
            return ctx.enter_context(nc.sbuf_tensor(name, shape, dt))

        W0, WH, W1, W2 = 0, 2 * C, 2 * C + HC, 3 * C + HC
        w_hi = sb("w_hi", [P, W2 + C, F], F32R)
        w_lo = sb("w_lo", [P, W2 + C, F], F32R)
        wo_hi = sb("wo_hi", [P, HC, F + 2], F32R)
        wo_lo = sb("wo_lo", [P, HC, F + 2], F32R)
        ad_hi = sb("ad_hi", [P, 2 * N], F32R)
        ad_lo = sb("ad_lo", [P, 2 * N], F32R)
        mask = sb("mask", [P, H, N], BF16)
        ident = sb("ident", [P, P])
        identb = sb("identb", [P, P], BF16)
        db = sb("db", [P, F])
        b2_all = sb("b2_all", [P, F])
        gamma_all = sb("gamma_all", [P, F])
        beta_all = sb("beta_all", [P, F])
        b1_col = sb("b1_col", [P, C])
        wa = sb("wa", [P, C, 2 * H])
        wao = sb("wao", [P, HC, 2])
        deg = sb("deg", [P, 1])
        stage = sb("stage", [P, 4 * C, F])

        x_in = sb("x_in", [P, 4, 2, F])
        x_hi = sb("x_hi", [P, 2, 2, F], F32R)
        x_lo = sb("x_lo", [P, 2, 2, F], F32R)
        ax_hi = sb("ax_hi", [P, 2, C, 2 * N], F32R)
        ax_lo = sb("ax_lo", [P, 2, C, 2 * N], F32R)
        v0 = sb("v0", [P, 2, F])
        x1 = sb("x1", [P, 2, 2, F])
        x1_hi = sb("x1_hi", [P, 2, 2, F], F32R)
        x1_lo = sb("x1_lo", [P, 2, 2, F], F32R)
        x1b = sb("x1b", [P, 4, 2, F])
        x1t = sb("x1t", [P, 2, C, N])
        f_sb = sb("f_sb", [P, 2, 2, H])
        f_rest = sb("f_rest", [P, 2, 2, H])
        s1 = sb("s1", [P, 2, 2, P + 3], BF16)
        t1_left = sb("t1_left", [P, 2, N], BF16)
        t1_right = sb("t1_right", [P, 2, H, N], BF16)
        att = sb("att", [P, 2, H, N])
        nm1 = sb("nm1", [P, 2, H])
        sm1 = sb("sm1", [P, 2, H])
        rc1 = sb("rc1", [P, 2, H])
        pt_hi = sb("pt_hi", [P, 2, H * N], F32R)
        pt_lo = sb("pt_lo", [P, 2, H * N], F32R)
        y_hi = sb("y_hi", [P, C, H, 2, N], F32R)
        y_lo = sb("y_lo", [P, C, H, 2, N], F32R)
        elu = sb("elu", [P, 2, C, 2 * N])
        hv = sb("hv", [P, 2, C, 2 * N])
        h_hi = sb("h_hi", [P, HC, 2, N], F32R)
        h_lo = sb("h_lo", [P, HC, 2, N], F32R)
        g_hi = sb("g_hi", [P, 2, 2, F], F32R)
        g_lo = sb("g_lo", [P, 2, 2, F], F32R)
        f2_sb = sb("f2_sb", [P, 2, 2])
        f2_rest = sb("f2_rest", [P, 2, 2])
        s2 = sb("s2", [P, 2, P + 3], BF16)
        t2_left = sb("t2_left", [P, N], BF16)
        t2_right = sb("t2_right", [P, 2, N], BF16)
        att2 = sb("att2", [P, 2, N])
        nm2 = sb("nm2", [P, 2])
        sm2 = sb("sm2", [P, 2])
        rc2 = sb("rc2", [P, 2])
        pt2_hi = sb("pt2_hi", [P, 2 * N], F32R)
        pt2_lo = sb("pt2_lo", [P, 2 * N], F32R)
        ov = sb("ov", [P, 2, F])
        oe = sb("oe", [P, 2, F])
        o_sb = sb("o_sb", [P, 2, F])
        ot_hi = sb("ot_hi", [P, C, 2 * N], F32R)
        ot_lo = sb("ot_lo", [P, C, 2 * N], F32R)
        d_sb = sb("d_sb", [P, C, 2 * N])
        d_hi = sb("d_hi", [P, C, 2 * N], F32R)
        d_lo = sb("d_lo", [P, C, 2 * N], F32R)
        r_sb = sb("r_sb", [P, 2, F])
        out_sb = sb("out_sb", [P, 2, 2, F])
        bn0, bn1, bn2 = (sb(f"bn{i}", [P, 2, 6]) for i in range(3))
        mv0, mv1, mv2 = (sb(f"mv{i}", [P, 2, 2]) for i in range(3))
        ve0, ve1, ve2 = (sb(f"ve{i}", [P, 2]) for i in range(3))
        eps_col = sb("eps_col", [P, 2])
        zeros = sb("zeros", [P, 2, 2, H])
        half_col = sb("half_col", [P, 2])
        rs0, rs1, rs2 = (sb(f"rs{i}", [P, 2]) for i in range(3))
        a_all = x1b[:, :, :, :].rearrange("p a b f -> p a (b f)")
        ao_all = r_sb[:, :, :]
        b0_all = out_sb[:, 0, 0, :]
        adj_i = out_sb[:, 0, 1, 0:N].bitcast(I32)
        adjt_i = out_sb[:, 0, 1, N:2 * N].bitcast(I32)
        adj_f = out_sb[:, 1, 0, 0:N]
        ad_f = out_sb[:, 1, 1, :]
        junk = v0[:, 0, :]

        bank = [ctx.enter_context(nc.psum_tensor(f"bank{i}", [P, 512], F32)) for i in range(8)]
        S2_BANK, AX_BANK, Z2_BANK, G_BANK, PT2_BANK, B_BANK, PT_BANK = 0, (1, 2), 3, (4, 6), 0, 5, (3, 1)
        O_BANK, E_BANK, C_BANK, TR_BANK, F_BANK, H_BANK = 2, (0, 4, 5, 3), 1, 2, 6, (7, 5, 2, 6)
        D1_BANK, S_BANK, Z_BANK, D2_BANK = 0, 4, (3, 1), 7

        sems = """
            w_in c_in w_hi w_lo wa0 wao mask_ones ident0 ident ad0 ad1 ad2 ad3 ad_done db
            x_hi x_lo x_db ax ax_hi ax_lo b v0 bn0 mv0 ve0 rs0 x1 x1_hi x1_lo x1b c x1t f f_sb
            s1a s1b s1c s1d s1 s1t t1 z l1 lm1 nm1 e1 rc1 pn pt pt_hi pt_lo
            y y_hi y_lo h h_e h_u h_v h_hi h_lo g g_hi g_lo f2
            s2a s2b s2c s2d s2 s2t t2 z2 l2 lm2 nm2 e2 rc2 pt2 pt2_hi pt2_lo o ov oe ou o_sb vb
            tr ot_hi ot_lo d1 relu d_hi d_lo d2 yv bn1 mv1 ve1 rs1 q r bn2 mv2 ve2 rs2 out
        """.split()
        S = {n: ctx.enter_context(nc.semaphore(f"{n}_s")) for n in sems}
        x_in_s = [ctx.enter_context(nc.semaphore(f"x_in{i}_s")) for i in range(4)]
        out_s = [ctx.enter_context(nc.semaphore(f"out{i}_s")) for i in range(4)]
        block = ctx.enter_context(nc.Block())

        def plain(r):
            return r.bitcast(F32)

        def x_arrived(eng, p):
            if p.there():
                eng.wait_ge(x_in_s[p.slot(4)], (p.turn + p.off // 4 + 1) * 16)

        @block.sync
        def _(sp):
            sp.dma_start(adj_i, adj).then_inc(S["c_in"], 16)
            sp.dma_start(adjt_i, adj_t).then_inc(S["c_in"], 16)
            sp.dma_start(b0_all, b0.partition_broadcast(P)).then_inc(S["c_in"], 16)
            sp.dma_start(b2_all[:, :], b2.partition_broadcast(P)).then_inc(S["c_in"], 16)
            sp.dma_start(gamma_all[:, :], gamma.partition_broadcast(P)).then_inc(S["c_in"], 16)
            sp.dma_start(beta_all[:, :], beta.partition_broadcast(P)).then_inc(S["c_in"], 16)
            sp.dma_start(b1_col[:, :], b1).then_inc(S["c_in"], 16)
            sp.dma_start(a_all, a_heads.partition_broadcast(P)).then_inc(S["c_in"], 16)
            sp.dma_start(ao_all, a_out.rearrange("(a f) -> a f", a=2).partition_broadcast(P)).then_inc(S["c_in"], 16)

            def load(p):
                after(sp, S["v0"], p.back(4))
                if p.there():
                    sp.dma_start(x_in[:, p.slot(4)], x_pairs[p.index()]).then_inc(x_in_s[p.slot(4)], 16)

            for t in range(3):
                load(Pair(0, t, PAIRS))
            sp.dma_start(stage[:, 0:2 * C], w0_t.rearrange("(c p) o -> p c o", p=P)).then_inc(S["w_in"], 16)
            sp.dma_start(stage[:, 2 * C:3 * C], w1.rearrange("(c p) o -> p c o", p=P)).then_inc(S["w_in"], 16)
            sp.dma_start(stage[:, 3 * C:4 * C], w2.rearrange("(c p) o -> p c o", p=P)).then_inc(S["w_in"], 16)
            sp.wait_ge(S["w_lo"], 1)
            sp.dma_start(stage[:, :], w_heads.rearrange("h (c p) o -> p (h c) o", p=P)).then_inc(S["w_in"], 16)
            sp.wait_ge(S["w_lo"], 2)
            sp.wait_ge(S["wa0"], 2 * HC)
            sp.dma_start(stage[:, :], w_out.rearrange("(c p) o -> p c o", p=P)).then_inc(S["w_in"], 16)

            def step(t):
                r = t.back(4)
                load(Pair(t.turn, t.off + 3, PAIRS))
                if r.there():
                    after(sp, S["out"], r, 2)
                    sp.dma_start(out_pairs[r.index()], out_sb[:, r.slot(2)]).then_inc(out_s[r.slot(4)], 16)

            over_steps(sp, PAIRS, step)
            for i in range(4):
                sp.wait_ge(out_s[i], 16 * (PAIRS // 4))

        @block.tensor
        def _(pe):
            def triple(ps, a_hi, a_lo, b_hi, b_lo, start, stop):
                nc.tensor.matmul(ps, a_hi, b_hi, start=start, stop=False)
                nc.tensor.matmul(ps, a_hi, b_lo, start=False, stop=False)
                return nc.tensor.matmul(ps, a_lo, b_hi, start=False, stop=stop)

            def ax_products(p, m, g):
                if not p.there():
                    return
                after(pe, S["x_hi"], p)
                after(pe, S["x_lo"], p)
                if p.off == 0:
                    pe.wait_ge(S["ad_done"], 2)
                i = p.slot(2)
                after(pe, S["lm1"], m, 2)
                after(pe, S["h_v"], g, H, 3)
                for b in range(2):
                    for c in range(C):
                        last = triple(bank[AX_BANK[b]][:, c * 2 * N:(c + 1) * 2 * N],
                                      x_hi[:, i, b, c * P:(c + 1) * P], x_lo[:, i, b, c * P:(c + 1) * P],
                                      ad_hi[:, :], ad_lo[:, :], c == 0, c == C - 1)
                    last.then_inc(S["ax"], 1)

            def y_products(m, u, g, p):
                if not m.there():
                    return
                b, c = u // C, u % C
                if c == 0:
                    after(pe, S["pt_hi"], m, 2, b + 1)
                    after(pe, S["pt_lo"], m, 2, b + 1)
                if u == 0:
                    after(pe, S["x1_hi"], m)
                    after(pe, S["x1_lo"], m)
                if u == 2:
                    after(pe, S["v0"], p)
                if u == 1:
                    after(pe, S["f2"], g, 2, 1)
                i = m.slot(2)
                triple(bank[E_BANK[u]][:, :], x1_hi[:, i, b, c * P:(c + 1) * P], x1_lo[:, i, b, c * P:(c + 1) * P],
                       pt_hi[:, b], pt_lo[:, b], True, True).then_inc(S["y"], 1)

            def s2_transposes(q):
                if not q.there():
                    return
                after(pe, S["s2"], q)
                ps = bank[S2_BANK][:, :].bitcast(BF16)
                for side in range(2):
                    last = nc.tensor.transpose(ps[:, side * N:(side + 1) * N],
                                               s2[:, :, :].rearrange("p s w -> p (s w)")[:, side * P:(side + 1) * P],
                                               identb[:, :])
                last.then_inc(S["s2t"], 1)

            def b_products(p):
                if not p.there():
                    return
                if p.off == 0:
                    pe.wait_ge(S["w_hi"], 1)
                    pe.wait_ge(S["w_lo"], 1)
                for b in range(2):
                    after(pe, S["ax_hi"], p, 2, b + 1)
                    after(pe, S["ax_lo"], p, 2, b + 1)
                    for k in range(2 * C):
                        side, c = k // C, k % C
                        cols = slice(N, 2 * N) if side == 0 else slice(0, N)
                        last = triple(bank[B_BANK][:, b * F:(b + 1) * F], ax_hi[:, b, c, cols], ax_lo[:, b, c, cols],
                                      w_hi[:, W0 + k], w_lo[:, W0 + k], k == 0, k == 2 * C - 1)
                last.then_inc(S["b"], 1)

            def z2_products(q):
                if not q.there():
                    return
                after(pe, S["t2"], q, 3)
                ps = bank[Z2_BANK]
                nc.tensor.matmul(ps[:, 0:2 * N], identb[:, :], mask[:, 0:2], start=True, stop=False)
                nc.tensor.matmul(ps[:, 0:2 * N], t2_left[:, :], t2_right[:, :, :], start=False, stop=True)\
                    .then_inc(S["z2"], 1)

            def g_products(g, b):
                if not g.there():
                    return
                if b == 0:
                    after(pe, S["h_hi"], g, H)
                    after(pe, S["h_lo"], g, H)
                    if g.off == 0:
                        pe.wait_ge(S["w_lo"], 3)
                        pe.wait_ge(S["w_hi"], 3)
                for k in range(HC):
                    last = triple(bank[G_BANK[b]][:, 0:F + 2], h_hi[:, k, b], h_lo[:, k, b], wo_hi[:, k], wo_lo[:, k],
                                  k == 0, k == HC - 1)
                last.then_inc(S["g"], 1)

            def c_transposes(p):
                if not p.there():
                    return
                after(pe, S["x1"], p, 2)
                for b in range(2):
                    for c in range(C):
                        k = b * C + c
                        last = nc.tensor.transpose(bank[C_BANK][:, k * N:(k + 1) * N],
                                                   x1[:, p.slot(2), b, c * P:(c + 1) * P], ident[:, :])
                last.then_inc(S["c"], 1)

            def pt2_transposes(q):
                if not q.there():
                    return
                after(pe, S["e2"], q)
                for b in range(2):
                    last = nc.tensor.transpose(bank[PT2_BANK][:, b * N:(b + 1) * N], att2[:, b], ident[:, :])
                last.then_inc(S["pt2"], 1)

            def f_products(p, g):
                if not p.there():
                    return
                after(pe, S["x1t"], p)
                after(pe, S["f2"], g, 2, 2)
                if p.off == 0:
                    pe.wait_ge(S["wa0"], 2 * HC)
                for b in range(2):
                    for c in range(C):
                        last = nc.tensor.matmul(bank[F_BANK][:, b * 2 * H:(b + 1) * 2 * H], x1t[:, b, c], wa[:, c],
                                                start=c == 0, stop=c == C - 1)
                last.then_inc(S["f"], 1)

            def o_products(q):
                if not q.there():
                    return
                after(pe, S["pt2_hi"], q)
                after(pe, S["pt2_lo"], q)
                for b in range(2):
                    last = triple(bank[O_BANK][:, b * F:(b + 1) * F], pt2_hi[:, b * N:(b + 1) * N],
                                  pt2_lo[:, b * N:(b + 1) * N], g_hi[:, q.slot(2), b], g_lo[:, q.slot(2), b], True, True)
                last.then_inc(S["o"], 1)

            def s_transposes(p):
                if not p.there():
                    return
                after(pe, S["s1"], p)
                ps = bank[S_BANK][:, :].bitcast(BF16)
                for b in range(2):
                    cols = s1[:, b].rearrange("p s w -> p (s w)")
                    for side in range(2):
                        k = 2 * b + side
                        last = nc.tensor.transpose(ps[:, k * N:(k + 1) * N], cols[:, side * P:(side + 1) * P],
                                                   identb[:, :])
                last.then_inc(S["s1t"], 1)

            def h_products(m, h, q):
                if not m.there():
                    return
                if h == 0:
                    after(pe, S["yv"], q.back(1))
                    after(pe, S["y_hi"], m, 4)
                    after(pe, S["y_lo"], m, 4)
                    if m.off == 0:
                        pe.wait_ge(S["w_hi"], 2)
                        pe.wait_ge(S["w_lo"], 2)
                for o in range(C):
                    for c in range(C):
                        k = WH + h * C + c
                        last = triple(bank[H_BANK[h]][:, o * 2 * N:(o + 1) * 2 * N], w_hi[:, k, o * P:(o + 1) * P],
                                      w_lo[:, k, o * P:(o + 1) * P], y_hi[:, c, h], y_lo[:, c, h],
                                      c == 0, c == C - 1)
                last.then_inc(S["h"], 1)

            def z_products(p):
                if not p.there():
                    return
                after(pe, S["t1"], p, H + 1)
                for b in range(2):
                    ps = bank[Z_BANK[b]]
                    nc.tensor.matmul(ps[:, :], identb[:, :], mask[:, :, :], start=True, stop=False)
                    nc.tensor.matmul(ps[:, :], t1_left[:, b], t1_right[:, b], start=False, stop=True)\
                        .then_inc(S["z"], 1)

            def o_transposes(q):
                if not q.there():
                    return
                after(pe, S["o_sb"], q)
                for b in range(2):
                    for c in range(C):
                        last = nc.tensor.transpose(bank[TR_BANK][:, (2 * c + b) * N:(2 * c + b + 1) * N],
                                                   o_sb[:, b, c * P:(c + 1) * P], ident[:, :])
                last.then_inc(S["tr"], 1)

            def d1_products(q):
                if not q.there():
                    return
                after(pe, S["ot_hi"], q)
                after(pe, S["ot_lo"], q)
                for d in range(C):
                    for c in range(C):
                        last = triple(bank[D1_BANK][:, d * 2 * N:(d + 1) * 2 * N], w_hi[:, W1 + c, d * P:(d + 1) * P],
                                      w_lo[:, W1 + c, d * P:(d + 1) * P], ot_hi[:, c], ot_lo[:, c],
                                      c == 0, c == C - 1)
                last.then_inc(S["d1"], 1)

            def d2_products(q, m):
                if not q.there():
                    return
                after(pe, S["d_hi"], q)
                after(pe, S["d_lo"], q)
                after(pe, S["h_v"], m, H, 1)
                for b in range(2):
                    for c in range(C):
                        last = triple(bank[D2_BANK][:, b * F:(b + 1) * F], d_hi[:, c, b * N:(b + 1) * N],
                                      d_lo[:, c, b * N:(b + 1) * N], w_hi[:, W2 + c], w_lo[:, W2 + c],
                                      c == 0, c == C - 1)
                last.then_inc(S["d2"], 1)

            def pt_transposes(p):
                if not p.there():
                    return
                for b in range(2):
                    after(pe, S["pn"], p, 2, b + 1)
                    for h in range(H):
                        last = nc.tensor.transpose(bank[PT_BANK[b]][:, h * N:(h + 1) * N], att[:, b, h], ident[:, :])
                    last.then_inc(S["pt"], 1)

            def step(t):
                p, m, g, q, r = (t.back(k) for k in range(5))
                s2_transposes(q)
                ax_products(p, m, g)
                z2_products(q)
                g_products(g, 0)
                b_products(p)
                pt2_transposes(q)
                pt_transposes(m)
                g_products(g, 1)
                o_products(q)
                y_products(m, 0, g, p)
                y_products(m, 1, g, p)
                y_products(m, 2, g, p)
                y_products(m, 3, g, p)
                c_transposes(p)
                o_transposes(q)
                f_products(p, g)
                h_products(m, 0, q)
                d1_products(q)
                s_transposes(p)
                h_products(m, 1, q)
                z_products(p)
                h_products(m, 2, q)
                h_products(m, 3, q)
                d2_products(q, m)

            pe.wait_ge(S["ident"], 2)
            over_steps(pe, PAIRS, step)

        @block.scalar
        def _(act):
            def split_weights(lot, src, hi):
                nc.scalar.activation(hi, src, ACT.Copy).then_inc(S["w_hi"], 1)

            act.wait_ge(S["mask_ones"], 1)
            act.wait_ge(S["w_in"], 16 * 3)
            hi_w = w_hi[:, :, :]
            nc.scalar.activation(hi_w[:, 0:2 * C], stage[:, 0:2 * C], ACT.Copy)
            nc.scalar.activation(hi_w[:, W1:W1 + 2 * C], stage[:, 2 * C:4 * C], ACT.Copy).then_inc(S["w_hi"], 1)
            act.wait_ge(S["w_in"], 16 * 4)
            nc.scalar.activation(hi_w[:, WH:WH + HC], stage[:, :], ACT.Copy).then_inc(S["w_hi"], 1)
            act.wait_ge(S["w_in"], 16 * 5)
            nc.scalar.activation(wo_hi[:, :, 0:F], stage[:, :], ACT.Copy)
            act.wait_ge(S["wao"], 2 * HC)
            nc.scalar.activation(wo_hi[:, :, F:F + 2], wao[:, :, :], ACT.Copy).then_inc(S["w_hi"], 1)

            def x_high(p):
                if p.there():
                    x_arrived(act, p)
                    nc.scalar.activation(x_hi[:, p.slot(2)], x_in[:, p.slot(4)], ACT.Copy).then_inc(S["x_hi"], 1)

            def pt_high(m, b):
                if m.there():
                    after(act, S["pt"], m, 2, b + 1)
                    nc.scalar.activation(pt_hi[:, b], bank[PT_BANK[b]][:, :], ACT.Copy).then_inc(S["pt_hi"], 1)

            def elu_exp(m, h):
                if m.there():
                    after(act, S["h"], m, H, h + 1)
                    if h < 2:
                        after(act, S["h_v"], m.back(1), H, h + 3)
                    else:
                        after(act, S["h_v"], m, H, h - 1)
                    nc.scalar.activation(elu[:, h % 2].rearrange("p c n -> p (c n)"), bank[H_BANK[h]][:, :],
                                         ACT.Exp).then_inc(S["h_e"], 1)

            def elu_high(m, h):
                if m.there():
                    after(act, S["h_v"], m, H, h + 1)
                    nc.scalar.activation(h_hi[:, h * C:(h + 1) * C].rearrange("p c b n -> p c (b n)"), hv[:, h % 2],
                                         ACT.Copy).then_inc(S["h_hi"], 1)

            def ax_high(p, b):
                if p.there():
                    after(act, S["ax"], p, 2, b + 1)
                    nc.scalar.activation(ax_hi[:, b].rearrange("p c n -> p (c n)"), bank[AX_BANK[b]][:, :],
                                         ACT.Copy).then_inc(S["ax_hi"], 1)

            def y_high(m, u):
                if m.there():
                    b, c = u // C, u % C
                    after(act, S["y"], m, 4, u + 1)
                    nc.scalar.activation(y_hi[:, c, :, b], bank[E_BANK[u]][:, :].rearrange("p (h n) -> p h n", h=H),
                                         ACT.Copy).then_inc(S["y_hi"], 1)

            def t2_copy(q):
                if q.there():
                    after(act, S["s2t"], q)
                    ps = bank[S2_BANK][:, :].bitcast(BF16)
                    nc.scalar.activation(t2_left[:, :], ps[:, 0:N], ACT.Copy).then_inc(S["t2"], 1)
                    for b in range(2):
                        rows = slice(32 * b, 32 * b + 32)
                        nc.scalar.activation(t2_right[rows, b], ps[rows, N:2 * N], ACT.Copy).then_inc(S["t2"], 1)

            def x1_high(p):
                if p.there():
                    after(act, S["x1"], p, 2)
                    nc.scalar.activation(x1_hi[:, p.slot(2)], x1[:, p.slot(2)], ACT.Copy).then_inc(S["x1_hi"], 1)

            def leaky2(q):
                if q.there():
                    after(act, S["z2"], q)
                    nc.scalar.activation(att2[:, :, :].rearrange("p b n -> p (b n)"), bank[Z2_BANK][:, 0:2 * N],
                                         ACT.Copy, scale=SLOPE).then_inc(S["l2"], 1)

            def exp2(q):
                if q.there():
                    after(act, S["nm2"], q)
                    for b in range(2):
                        last = nc.scalar.activation(att2[:, b], att2[:, b], ACT.Exp, bias=nm2[:, b:b + 1],
                                                    accum_out=sm2[:, b:b + 1])
                    last.then_inc(S["e2"], 1)

            def g_high(g, b):
                if g.there():
                    after(act, S["g"], g, 2, b + 1)
                    nc.scalar.activation(g_hi[:, g.slot(2), b], bank[G_BANK[b]][:, 0:F], ACT.Copy).then_inc(S["g_hi"], 1)

            def x1t_copy(p):
                if p.there():
                    after(act, S["c"], p)
                    nc.scalar.activation(x1t[:, :, :, :].rearrange("p b c n -> p (b c n)"), bank[C_BANK][:, :],
                                         ACT.Copy).then_inc(S["x1t"], 1)

            def pt2_high(q):
                if q.there():
                    after(act, S["pt2"], q)
                    nc.scalar.activation(pt2_hi[:, :], bank[PT2_BANK][:, 0:2 * N], ACT.Copy).then_inc(S["pt2_hi"], 1)

            def o_values(q):
                if q.there():
                    after(act, S["o"], q)
                    after(act, S["rc2"], q)
                    for b in range(2):
                        last = nc.scalar.activation(ov[:, b], bank[O_BANK][:, b * F:(b + 1) * F], ACT.Copy,
                                                    scale=rc2[:, b:b + 1])
                    last.then_inc(S["ov"], 1)

            def o_exp(q):
                if q.there():
                    after(act, S["ov"], q)
                    nc.scalar.activation(oe[:, :, :], ov[:, :, :], ACT.Exp).then_inc(S["oe"], 1)

            def t1_copy(p):
                if p.there():
                    after(act, S["s1t"], p)
                    ps = bank[S_BANK][:, :].bitcast(BF16)[:, 0:4 * N].rearrange("p (b s n) -> p b s n", b=2, s=2)
                    nc.scalar.activation(t1_left[:, :, :], ps[:, :, 0], ACT.Copy).then_inc(S["t1"], 1)
                    for h in range(H):
                        rows = slice(32 * h, 32 * h + 32)
                        nc.scalar.activation(t1_right[rows, :, h], ps[rows, :, 1], ACT.Copy).then_inc(S["t1"], 1)

            def leaky1(p, b):
                if p.there():
                    after(act, S["z"], p, 2, b + 1)
                    nc.scalar.activation(att[:, b].rearrange("p h n -> p (h n)"), bank[Z_BANK[b]][:, :], ACT.Copy,
                                         scale=SLOPE).then_inc(S["l1"], 1)

            def exp1(p, b):
                if p.there():
                    after(act, S["nm1"], p, 2, b + 1)
                    for h in range(H):
                        last = nc.scalar.activation(att[:, b, h], att[:, b, h], ACT.Exp, bias=nm1[:, b, h:h + 1],
                                                    accum_out=sm1[:, b, h:h + 1])
                    last.then_inc(S["e1"], 1)

            def ot_high(q):
                if q.there():
                    after(act, S["tr"], q)
                    nc.scalar.activation(ot_hi[:, :, :].rearrange("p c n -> p (c n)"), bank[TR_BANK][:, :],
                                         ACT.Copy).then_inc(S["ot_hi"], 1)

            def d_relu(q):
                if q.there():
                    after(act, S["d1"], q)
                    for d in range(C):
                        nc.scalar.activation(d_sb[:, d], bank[D1_BANK][:, d * 2 * N:(d + 1) * 2 * N], ACT.Relu,
                                             bias=b1_col[:, d:d + 1]).then_inc(S["relu"], 1)

            def d_high(q):
                if q.there():
                    after(act, S["relu"], q, 2)
                    nc.scalar.activation(d_hi[:, :, :], d_sb[:, :, :], ACT.Copy).then_inc(S["d_hi"], 1)

            def step(t):
                p, m, g, q, r = (t.back(k) for k in range(5))
                t2_copy(q)
                ax_high(p, 0)
                leaky2(q)
                ax_high(p, 1)
                exp1(m, 0)
                exp2(q)
                exp1(m, 1)
                g_high(g, 0)
                pt2_high(q)
                pt_high(m, 0)
                pt_high(m, 1)
                x_high(Pair(t.turn, t.off + 1, PAIRS))
                g_high(g, 1)
                o_values(q)
                y_high(m, 0)
                o_exp(q)
                y_high(m, 1)
                y_high(m, 2)
                y_high(m, 3)
                x1t_copy(p)
                ot_high(q)
                x1_high(p)
                elu_exp(m, 0)
                d_relu(q)
                d_high(q)
                elu_high(m, 0)
                t1_copy(p)
                elu_exp(m, 1)
                elu_high(m, 1)
                leaky1(p, 0)
                leaky1(p, 1)
                elu_exp(m, 2)
                elu_high(m, 2)
                elu_exp(m, 3)
                elu_high(m, 3)

            x_high(Pair(0, 0, PAIRS))
            over_steps(act, PAIRS, step)

        @block.vector
        def _(dve):
            dve.wait_ge(S["c_in"], 16 * 9)
            nc.vector.tensor_copy(adj_f, adj_i)
            nc.vector.tensor_copy(ad_f[:, 0:N], adjt_i).then_inc(S["ad0"], 1)
            dve.wait_ge(S["ad0"], 1)
            nc.vector.reduce_sum(deg[:, :], adj_f, AX_X).then_inc(S["ad1"], 1)
            for h in range(H):
                nc.vector.tensor_scalar(mask[:, h], adj_f, 0.0, MASKED, ALU.is_le, ALU.mult)
            dve.wait_ge(S["ad1"], 1)
            dve.wait_ge(S["ident"], 2)
            nc.vector.tensor_scalar(ad_f[:, N:2 * N], ident[:, :], deg[:, 0:1], None, ALU.mult).then_inc(S["ad2"], 1)
            nc.vector.tensor_scalar(db[:, :], b0_all, deg[:, 0:1], None, ALU.mult).then_inc(S["db"], 1)
            dve.wait_ge(S["ad2"], 1)
            nc.vector.tensor_copy(ad_hi[:, :], ad_f).then_inc(S["ad3"], 1)
            dve.wait_ge(S["ad3"], 1)
            nc.vector.tensor_tensor(ad_lo[:, :], ad_f, plain(ad_hi[:, :]), ALU.subtract).then_inc(S["ad_done"], 2)

            dve.wait_ge(S["w_hi"], 1)
            nc.vector.tensor_tensor(w_lo[:, 0:2 * C], stage[:, 0:2 * C], plain(w_hi[:, 0:2 * C]), ALU.subtract)
            nc.vector.tensor_tensor(w_lo[:, W1:W1 + 2 * C], stage[:, 2 * C:4 * C], plain(w_hi[:, W1:W1 + 2 * C]),
                                    ALU.subtract).then_inc(S["w_lo"], 1)
            dve.wait_ge(S["w_hi"], 2)
            nc.vector.tensor_tensor(w_lo[:, WH:WH + HC], stage[:, :], plain(w_hi[:, WH:WH + HC]),
                                    ALU.subtract).then_inc(S["w_lo"], 1)
            done = 0
            for h in range(H):
                for c in range(C):
                    for side in range(2):
                        if done:
                            dve.wait_ge(S["wa0"], done)
                        nc.vector.tensor_tensor_reduce(junk, stage[:, h * C + c], a_all[:, h, side * F:(side + 1) * F],
                                                       1.0, 0.0, ALU.mult, ALU.add,
                                                       wa[:, c, side * H + h:side * H + h + 1]).then_inc(S["wa0"], 1)
                        done += 1
            done = 0
            dve.wait_ge(S["w_in"], 16 * 5)
            for k in range(HC):
                for side in range(2):
                    dve.wait_ge(S["wao"], done) if done else dve.wait_ge(S["wa0"], 2 * HC)
                    nc.vector.tensor_tensor_reduce(junk, stage[:, k], ao_all[:, side], 1.0, 0.0, ALU.mult, ALU.add,
                                                   wao[:, k, side:side + 1]).then_inc(S["wao"], 1)
                    done += 1
            dve.wait_ge(S["w_hi"], 3)
            dve.wait_ge(S["wao"], 2 * HC)
            nc.vector.tensor_tensor(wo_lo[:, :, 0:F], stage[:, :], plain(wo_hi[:, :, 0:F]), ALU.subtract)
            nc.vector.tensor_tensor(wo_lo[:, :, F:F + 2], wao[:, :, :], plain(wo_hi[:, :, F:F + 2]),
                                    ALU.subtract).then_inc(S["w_lo"], 1)

            def pt_low(m, b):
                if m.there():
                    after(dve, S["pt_hi"], m, 2, b + 1)
                    nc.vector.tensor_tensor(pt_lo[:, b], bank[PT_BANK[b]][:, :], plain(pt_hi[:, b]),
                                            ALU.subtract).then_inc(S["pt_lo"], 1)

            def elu_values(m, h):
                if m.there():
                    i = h % 2
                    after(dve, S["h_e"], m, H, h + 1)
                    nc.vector.tensor_scalar(elu[:, i], elu[:, i], 1.0, -1.0, ALU.min, ALU.add).then_inc(S["h_u"], 1)
                    after(dve, S["h_u"], m, H, h + 1)
                    if h < 2:
                        after(dve, S["h_lo"], m.back(1), H, h + 3)
                    else:
                        after(dve, S["h_lo"], m, H, h - 1)
                    nc.vector.scalar_tensor_tensor(out=hv[:, i].rearrange("p c n -> p (c n)"), in0=bank[H_BANK[h]][:, :],
                                                   scalar=0.0, in1=elu[:, i].rearrange("p c n -> p (c n)"),
                                                   op0=ALU.max, op1=ALU.add).then_inc(S["h_v"], 1)

            def ax_low(p, b):
                if p.there():
                    after(dve, S["ax_hi"], p, 2, b + 1)
                    nc.vector.tensor_tensor(ax_lo[:, b].rearrange("p c n -> p (c n)"), bank[AX_BANK[b]][:, :],
                                            plain(ax_hi[:, b].rearrange("p c n -> p (c n)")),
                                            ALU.subtract).then_inc(S["ax_lo"], 1)

            def y_low(m, u):
                if m.there():
                    b, c = u // C, u % C
                    after(dve, S["y_hi"], m, 4, u + 1)
                    nc.vector.tensor_tensor(y_lo[:, c, :, b], bank[E_BANK[u]][:, :].rearrange("p (h n) -> p h n", h=H),
                                            plain(y_hi[:, c, :, b]), ALU.subtract).then_inc(S["y_lo"], 1)

            def statistics(src, bn, bn_s):
                for b in range(2):
                    last = nc.vector.bn_stats(bn[:, b], src[:, b])
                last.then_inc(bn_s, 1)

            def moments(t, bn, mv, bn_s, mv_s, between):
                after(dve, bn_s, t)
                between()
                if not t.there():
                    return
                for b in range(2):
                    last = nc.vector.bn_aggr(mv[:, b], bn[:, b])
                last.then_inc(mv_s, 1)

            def first_norm(p):
                if p.there():
                    i = p.slot(2)
                    after(dve, S["b"], p)
                    after(dve, S["x_db"], p)
                    nc.vector.tensor_tensor(v0[:, :, :].rearrange("p b f -> p (b f)"), bank[B_BANK][:, :],
                                            x_in[:, p.slot(4)].rearrange("p b f -> p (b f)"),
                                            ALU.add).then_inc(S["v0"], 1)
                    after(dve, S["v0"], p)
                    statistics(v0, bn0, S["bn0"])

            def first_scaled(p):
                if p.there():
                    i = p.slot(2)
                    after(dve, S["rs0"], p)
                    for b in range(2):
                        nc.vector.tensor_scalar(x1[:, i, b], v0[:, b], mv0[:, b, 0:1], rs0[:, b:b + 1],
                                                ALU.subtract, ALU.mult).then_inc(S["x1"], 1)

            def max2(q):
                if q.there():
                    after(dve, S["l2"], q)
                    flat = att2[:, :, :].rearrange("p b n -> p (b n)")
                    nc.vector.tensor_tensor(flat, bank[Z2_BANK][:, 0:2 * N], flat, ALU.max).then_inc(S["lm2"], 1)
                    after(dve, S["lm2"], q)
                    nc.vector.tensor_reduce(nm2[:, :], att2[:, :, :], AX_X, ALU.max, negate=True).then_inc(S["nm2"], 1)

            def g_low(g, b):
                if g.there():
                    after(dve, S["g_hi"], g, 2, b + 1)
                    i = g.slot(2)
                    nc.vector.tensor_tensor(g_lo[:, i, b], bank[G_BANK[b]][:, 0:F], plain(g_hi[:, i, b]),
                                            ALU.subtract).then_inc(S["g_lo"], 1)
                    if b == 0:
                        after(dve, S["s2"], g.back(1))
                    nc.vector.tensor_copy(f2_sb[:, b], bank[G_BANK[b]][:, F:F + 2]).then_inc(S["f2"], 1)

            def reciprocal2(q):
                if q.there():
                    after(dve, S["e2"], q)
                    nc.vector.reciprocal(rc2[:, :], sm2[:, :]).then_inc(S["rc2"], 1)

            def f_copy(p):
                if p.there():
                    after(dve, S["f"], p)
                    after(dve, S["s1"], p.back(1))
                    nc.vector.tensor_copy(f_sb[:, :, :, :].rearrange("p b s h -> p (b s h)"),
                                          bank[F_BANK][:, 0:4 * H]).then_inc(S["f_sb"], 1)

            def pt2_low(q):
                if q.there():
                    after(dve, S["pt2_hi"], q)
                    nc.vector.tensor_tensor(pt2_lo[:, :], bank[PT2_BANK][:, 0:2 * N], plain(pt2_hi[:, :]),
                                            ALU.subtract).then_inc(S["pt2_lo"], 1)

            def o_elu(q):
                if q.there():
                    after(dve, S["oe"], q)
                    nc.vector.tensor_scalar(oe[:, :, :], oe[:, :, :], 1.0, -1.0, ALU.min, ALU.add).then_inc(S["ou"], 1)
                    after(dve, S["ou"], q)
                    nc.vector.scalar_tensor_tensor(out=o_sb[:, :, :], in0=ov[:, :, :], scalar=0.0, in1=oe[:, :, :],
                                                   op0=ALU.max, op1=ALU.add).then_inc(S["o_sb"], 1)

            def max1(p, b):
                if p.there():
                    after(dve, S["l1"], p, 2, b + 1)
                    flat = att[:, b].rearrange("p h n -> p (h n)")
                    nc.vector.tensor_tensor(flat, bank[Z_BANK[b]][:, :], flat, ALU.max).then_inc(S["lm1"], 1)
                    after(dve, S["lm1"], p, 2, b + 1)
                    nc.vector.tensor_reduce(nm1[:, b], att[:, b], AX_X, ALU.max, negate=True).then_inc(S["nm1"], 1)

            def reciprocal1(p, b):
                if p.there():
                    after(dve, S["e1"], p, 2, b + 1)
                    nc.vector.reciprocal(rc1[:, b], sm1[:, b]).then_inc(S["rc1"], 1)

            def ot_low(q):
                if q.there():
                    after(dve, S["ot_hi"], q)
                    nc.vector.tensor_tensor(ot_lo[:, :, :].rearrange("p c n -> p (c n)"), bank[TR_BANK][:, :],
                                            plain(ot_hi[:, :, :].rearrange("p c n -> p (c n)")),
                                            ALU.subtract).then_inc(S["ot_lo"], 1)

            def norm_start(q):
                if not q.there():
                    return
                after(dve, S["d2"], q)
                after(dve, S["vb"], q)
                nc.vector.tensor_tensor(r_sb[:, :, :].rearrange("p b f -> p (b f)"), bank[D2_BANK][:, :],
                                        ov[:, :, :].rearrange("p b f -> p (b f)"), ALU.add).then_inc(S["yv"], 1)
                after(dve, S["yv"], q)
                statistics(r_sb, bn1, S["bn1"])

            def norm_scaled(q):
                if not q.there():
                    return
                after(dve, S["mv1"], q)
                for b in range(2):
                    last = nc.vector.scalar_tensor_tensor(out=r_sb[:, b], in0=r_sb[:, b], scalar=mv1[:, b, 0:1],
                                                          in1=gamma_all[:, :], op0=ALU.subtract, op1=ALU.mult)
                last.then_inc(S["q"], 1)
                after(dve, S["q"], q)
                after(dve, S["rs1"], q)
                for b in range(2):
                    last = nc.vector.scalar_tensor_tensor(out=r_sb[:, b], in0=r_sb[:, b], scalar=rs1[:, b:b + 1],
                                                          in1=x1b[:, q.slot(4), b], op0=ALU.mult, op1=ALU.add)
                last.then_inc(S["r"], 1)

            def last_statistics(q):
                if q.there():
                    after(dve, S["r"], q)
                    statistics(r_sb, bn2, S["bn2"])

            def norm_end(q):
                if not q.there():
                    return
                i = q.slot(2)
                after(dve, S["rs2"], q)
                before = q.back(2)
                if before.there():
                    dve.wait_ge(out_s[before.slot(4)], (before.turn + before.off // 4 + 1) * 16)
                for b in range(2):
                    nc.vector.tensor_scalar(out_sb[:, i, b], r_sb[:, b], mv2[:, b, 0:1], rs2[:, b:b + 1],
                                            ALU.subtract, ALU.mult).then_inc(S["out"], 1)

            def step(t):
                p, m, g, q, r = (t.back(k) for k in range(5))
                norm_start(r)
                moments(r, bn1, mv1, S["bn1"], S["mv1"], lambda: ax_low(p, 0))
                max2(q)
                ax_low(p, 1)
                norm_scaled(r)
                reciprocal1(m, 0)
                last_statistics(r)
                moments(r, bn2, mv2, S["bn2"], S["mv2"], lambda: reciprocal2(q))
                g_low(g, 0)
                reciprocal1(m, 1)
                pt2_low(q)
                first_norm(p)
                moments(p, bn0, mv0, S["bn0"], S["mv0"], lambda: pt_low(m, 0))
                pt_low(m, 1)
                norm_end(r)
                g_low(g, 1)
                first_scaled(p)
                y_low(m, 0)
                o_elu(q)
                y_low(m, 1)
                y_low(m, 2)
                y_low(m, 3)
                ot_low(q)
                f_copy(p)
                elu_values(m, 0)
                elu_values(m, 1)
                max1(p, 0)
                elu_values(m, 2)
                max1(p, 1)
                elu_values(m, 3)

            over_steps(dve, PAIRS, step)

        @block.gpsimd
        def _(pool):
            for m in (ident, identb):
                nc.gpsimd.memset(m[:, :], 0.0).then_inc(S["ident0"], 1)
            pool.wait_ge(S["ident0"], 2)
            for m in (ident, identb):
                nc.gpsimd.affine_select(out=m[:, :], in_=m[:, :], compare_op=ALU.not_equal, fill=1.0, base=0,
                                        pattern=[[-1, P]], channel_multiplier=1).then_inc(S["ident"], 1)
            nc.gpsimd.memset(eps_col[:, :], EPS)
            nc.gpsimd.memset(half_col[:, :], -0.5)
            nc.gpsimd.memset(zeros[:, :, :, :], 0.0)
            nc.gpsimd.memset(t1_right[:, :, :, :], 0.0)
            nc.gpsimd.memset(t2_right[:, :, :], 0.0)
            nc.gpsimd.memset(s1[:, :, :, :], 0.0)
            nc.gpsimd.memset(s2[:, :, :], 0.0).then_inc(S["mask_ones"], 1)
            pool.wait_ge(S["mask_ones"], 1)
            s1_groups = s1[:, :, :, 0:P].rearrange("p b s (h w) -> p b s h w", h=H)
            s1_flat = s1[:, :, :, :].rearrange("p b s w -> p b (s w)")
            s2_groups = s2[:, :, 0:64].rearrange("p s (b w) -> p s b w", b=2)
            s2_flat = s2[:, :, :].rearrange("p s w -> p (s w)")
            for side, first in ((0, 3), (1, 0)):
                ones1 = s1_flat[:, :, side * P:(side + 1) * P].rearrange("p b (h w) -> p b h w", h=H)
                for b in range(2):
                    nc.gpsimd.memset(ones1[:, b, :, first:first + 3], 1.0)
                ones2 = s2_flat[:, side * P:side * P + 64].rearrange("p (b w) -> p b w", b=2)
                last = nc.gpsimd.memset(ones2[:, :, first:first + 3], 1.0)
            last.then_inc(S["mask_ones"], 1)
            pool.wait_ge(S["mask_ones"], 2)
            pool.wait_ge(S["db"], 1)

            def x_low(p):
                if p.there():
                    i, k = p.slot(2), p.slot(4)
                    after(pool, S["x_hi"], p)
                    nc.gpsimd.tensor_tensor(x_lo[:, i], x_in[:, k], plain(x_hi[:, i]), ALU.subtract)\
                        .then_inc(S["x_lo"], 1)

            def x_bias(p):
                if p.there():
                    k = p.slot(4)
                    after(pool, S["x_lo"], p)
                    nc.gpsimd.tensor_tensor(x_in[:, k], x_in[:, k], db[:, :].unsqueeze(1).to_broadcast([P, 2, F]),
                                            ALU.add).then_inc(S["x_db"], 1)

            def h_low(m, h):
                if m.there():
                    after(pool, S["h_hi"], m, H, h + 1)
                    hc = slice(h * C, (h + 1) * C)
                    nc.gpsimd.tensor_tensor(h_lo[:, hc].rearrange("p c b n -> p c (b n)"), hv[:, h % 2],
                                            plain(h_hi[:, hc]).rearrange("p c b n -> p c (b n)"),
                                            ALU.subtract).then_inc(S["h_lo"], 1)

            def x1_beta(p):
                if p.there():
                    after(pool, S["x1"], p, 2)
                    after(pool, S["r"], p.back(4))
                    nc.gpsimd.tensor_tensor(x1b[:, p.slot(4)], x1[:, p.slot(2)],
                                            beta_all[:, :].unsqueeze(1).to_broadcast([P, 2, F]),
                                            ALU.add).then_inc(S["x1b"], 1)

            def x1_low(p):
                if p.there():
                    i = p.slot(2)
                    after(pool, S["x1_hi"], p)
                    nc.gpsimd.tensor_tensor(x1_lo[:, i], x1[:, i], plain(x1_hi[:, i]), ALU.subtract)\
                        .then_inc(S["x1_lo"], 1)

            def three_parts(t, src, rest, zero, parts, sa, sb_, sc, sd, se):
                nc.gpsimd.tensor_tensor(parts(0), src, zero, ALU.add).then_inc(sa, 1)
                after(pool, sa, t)
                nc.gpsimd.tensor_tensor(rest, src, parts(0), ALU.subtract).then_inc(sb_, 1)
                after(pool, sb_, t)
                nc.gpsimd.tensor_tensor(parts(1), rest, zero, ALU.add).then_inc(sc, 1)
                after(pool, sc, t)
                nc.gpsimd.tensor_tensor(rest, rest, parts(1), ALU.subtract).then_inc(sd, 1)
                after(pool, sd, t)
                nc.gpsimd.tensor_tensor(parts(2), rest, zero, ALU.add).then_inc(se, 1)

            def s1_parts(p):
                if p.there():
                    after(pool, S["f_sb"], p)
                    after(pool, S["s1t"], p.back(1))
                    three_parts(p, f_sb[:, :, :, :], f_rest[:, :, :, :], zeros[:, :, :, :], lambda k: s1_groups[:, :, :, :, k],
                                S["s1a"], S["s1b"], S["s1c"], S["s1d"], S["s1"])

            def s2_parts(g):
                if g.there():
                    after(pool, S["f2"], g, 2)
                    after(pool, S["s2t"], g.back(1))
                    three_parts(g, f2_sb[:, :, :].rearrange("p b s -> p s b"),
                                f2_rest[:, :, :].rearrange("p b s -> p s b"), zeros[:, :, :, 0], lambda k: s2_groups[:, :, :, k],
                                S["s2a"], S["s2b"], S["s2c"], S["s2d"], S["s2"])

            def scales(t, mv, ve, rs, mv_s, ve_s, rs_s):
                if t.there():
                    after(pool, mv_s, t)
                    nc.gpsimd.tensor_tensor(ve[:, :], mv[:, :, 1], eps_col[:, :], ALU.add).then_inc(ve_s, 1)
                    after(pool, ve_s, t)
                    nc.gpsimd.tensor_tensor(rs[:, :], ve[:, :], half_col[:, :], ALU.pow).then_inc(rs_s, 1)

            def ffn_bias(q):
                if q.there():
                    after(pool, S["o_sb"], q)
                    nc.gpsimd.tensor_tensor(ov[:, :, :], o_sb[:, :, :],
                                            b2_all[:, :].unsqueeze(1).to_broadcast([P, 2, F]),
                                            ALU.add).then_inc(S["vb"], 1)

            def probabilities(p, b):
                if p.there():
                    after(pool, S["rc1"], p, 2, b + 1)
                    nc.gpsimd.tensor_tensor(att[:, b], att[:, b], rc1[:, b].unsqueeze(2).to_broadcast([P, H, N]),
                                            ALU.mult).then_inc(S["pn"], 1)

            def d_low(q):
                if q.there():
                    after(pool, S["d_hi"], q)
                    nc.gpsimd.tensor_tensor(d_lo[:, :, :], d_sb[:, :, :], plain(d_hi[:, :, :]),
                                            ALU.subtract).then_inc(S["d_lo"], 1)

            def step(t):
                p, m, g, q, r = (t.back(k) for k in range(5))
                h_low(g, 3)
                scales(r, mv1, ve1, rs1, S["mv1"], S["ve1"], S["rs1"])
                x_bias(p)
                probabilities(m, 0)
                scales(r, mv2, ve2, rs2, S["mv2"], S["ve2"], S["rs2"])
                probabilities(m, 1)
                scales(p, mv0, ve0, rs0, S["mv0"], S["ve0"], S["rs0"])
                x_low(Pair(t.turn, t.off + 1, PAIRS))
                s2_parts(g)
                x1_beta(p)
                ffn_bias(q)
                s1_parts(p)
                x1_low(p)
                h_low(m, 0)
                d_low(q)
                h_low(m, 1)
                h_low(m, 2)

            x_low(Pair(0, 0, PAIRS))
            over_steps(pool, PAIRS, step)


def kernel(x, adj, L0_gnn_W, L0_gnn_b, L1_gnn_W_heads, L1_gnn_a_heads, L1_gnn_W_out, L1_gnn_a_out, L1_gnn_w1,
           L1_gnn_b1, L1_gnn_w2, L1_gnn_b2, L1_gnn_ln_gamma, L1_gnn_ln_beta):
    import concourse.bacc as bacc
    import numpy as np
    from concourse.bass_utils import run_bass_kernel_spmd

    nc = bacc.Bacc("TRN2", target_bir_lowering=False, num_devices=1)
    laid_out = {
        "x": x, "adj": adj, "adj_t": np.asarray(adj).T, "w0_t": np.asarray(L0_gnn_W).T, "b0": L0_gnn_b,
        "w_heads": L1_gnn_W_heads, "a_heads": L1_gnn_a_heads, "w_out": L1_gnn_W_out, "a_out": L1_gnn_a_out,
        "w1": L1_gnn_w1, "b1": np.asarray(L1_gnn_b1).reshape(2, 128).T, "w2": L1_gnn_w2, "b2": L1_gnn_b2, "gamma": L1_gnn_ln_gamma,
        "beta": L1_gnn_ln_beta,
    }
    arrays, args = {}, []
    for name, a in laid_out.items():
        a = np.ascontiguousarray(a)
        arrays[f"in_{name}"] = a
        args.append(nc.dram_tensor(f"in_{name}", a.shape, mybir.dt.from_np(a.dtype), kind="ExternalInput").ap())
    args.append(nc.dram_tensor("out_x", arrays["in_x"].shape, F32, kind="ExternalOutput").ap())
    graph_layers(nc, *args)
    r = run_bass_kernel_spmd(nc, [arrays], core_ids=[0])
    return r.results[0]["out_x"]
```

```python
from contextlib import ExitStack

import concourse.bass as bass
from concourse import mybir

ALU = mybir.AluOpType
ACT = mybir.ActivationFunctionType
F32 = mybir.dt.float32
F32R = mybir.dt.float32r
BF16 = mybir.dt.bfloat16
I32 = mybir.dt.int32
AX_X = mybir.AxisListType.X

P = 128
UNROLL = 4
LAST_STAGE = 5
REACH = 7
AHEAD = 3
MASKED = -float(2**100)
EPS = 1e-5
SLOPE = 0.01


class Pair:

    def __init__(self, turn, off, pairs):
        self.turn, self.off, self.pairs = turn, off, pairs

    def back(self, k):
        return Pair(self.turn, self.off - k, self.pairs)

    def there(self):
        return not isinstance(self.turn, int) or 0 <= self.off < self.pairs

    def slot(self, n):
        return self.off % n

    def index(self):
        return self.turn * UNROLL + self.off

    def count(self, per, k):
        return self.turn * (UNROLL * per) + (self.off * per + k)


def after(eng, sem, pair, per=1, k=None):
    if pair.there():
        eng.wait_ge(sem, pair.count(per, per if k is None else k))


def over_steps(eng, pairs, step):
    full = (pairs - REACH - AHEAD) // UNROLL
    for t in range(REACH):
        step(Pair(0, t, pairs))
    with eng.Fori(0, full) as turn:
        for j in range(UNROLL):
            step(Pair(turn, REACH + j, pairs))
    for t in range(REACH + UNROLL * full, pairs + LAST_STAGE):
        step(Pair(0, t, pairs))


def graph_layers(nc, x, adj, adj_t, w0_t, b0, w_heads, a_heads, w_out, a_out, w1, b1, w2, b2, gamma, beta, out):
    graphs, N, F = x.shape
    H = a_heads.shape[0]
    C = F // P
    PAIRS = graphs // 2
    HC = H * C
    assert N == P and F == 2 * P and H == 4 and graphs % 2 == 0

    x_pairs = x.rearrange("(p b) n f -> p n b f", b=2)
    out_pairs = out.rearrange("(p b) n f -> p n b f", b=2)

    with ExitStack() as ctx:
        def sb(name, shape, dt=F32):
            return ctx.enter_context(nc.sbuf_tensor(name, shape, dt))

        W0, WH, W1, W2 = 0, 2 * C, 2 * C + HC, 3 * C + HC
        w_hi = sb("w_hi", [P, W2 + C, F], F32R)
        w_lo = sb("w_lo", [P, W2 + C, F], F32R)
        wo_hi = sb("wo_hi", [P, HC, F + 2], F32R)
        wo_lo = sb("wo_lo", [P, HC, F + 2], F32R)
        ad_hi = sb("ad_hi", [P, 2 * N], F32R)
        ad_lo = sb("ad_lo", [P, 2 * N], F32R)
        mask = sb("mask", [P, H, N], BF16)
        ident = sb("ident", [P, P])
        identb = sb("identb", [P, P], BF16)
        db = sb("db", [P, F])
        b2_all = sb("b2_all", [P, F])
        gamma_all = sb("gamma_all", [P, F])
        beta_all = sb("beta_all", [P, F])
        b1_col = sb("b1_col", [P, C])
        wa = sb("wa", [P, C, 2 * H])
        wao = sb("wao", [P, HC, 2])
        deg = sb("deg", [P, 1])
        stage = sb("stage", [P, 4 * C, F])

        x_in = sb("x_in", [P, 4, 2, F])
        x_hi = sb("x_hi", [P, 2, 2, F], F32R)
        x_lo = sb("x_lo", [P, 2, 2, F], F32R)
        ax_hi = sb("ax_hi", [P, 2, C, 2 * N], F32R)
        ax_lo = sb("ax_lo", [P, 2, C, 2 * N], F32R)
        v0 = sb("v0", [P, 2, F])
        x1 = sb("x1", [P, 2, 2, F])
        x1_hi = sb("x1_hi", [P, 2, 2, F], F32R)
        x1_lo = sb("x1_lo", [P, 2, 2, F], F32R)
        x1b = sb("x1b", [P, 4, 2, F])
        x1t = sb("x1t", [P, 2, C, N])
        f_sb = sb("f_sb", [P, 2, 2, H])
        f_rest = sb("f_rest", [P, 2, 2, H])
        s1 = sb("s1", [P, 2, 2, P + 3], BF16)
        t1_left = sb("t1_left", [P, 2, N], BF16)
        t1_right = sb("t1_right", [P, 2, H, N], BF16)
        att = sb("att", [P, 2, H, N])
        nm1 = sb("nm1", [P, 2, H])
        sm1 = sb("sm1", [P, 2, H])
        rc1 = sb("rc1", [P, 2, H])
        pt_hi = sb("pt_hi", [P, 2, H * N], F32R)
        pt_lo = sb("pt_lo", [P, 2, H * N], F32R)
        y_hi = sb("y_hi", [P, C, H, 2, N], F32R)
        y_lo = sb("y_lo", [P, C, H, 2, N], F32R)
        elu = sb("elu", [P, 2, C, 2 * N])
        hv = sb("hv", [P, 2, C, 2 * N])
        h_hi = sb("h_hi", [P, HC, 2, N], F32R)
        h_lo = sb("h_lo", [P, HC, 2, N], F32R)
        g_hi = sb("g_hi", [P, 2, 2, F], F32R)
        g_lo = sb("g_lo", [P, 2, 2, F], F32R)
        f2_sb = sb("f2_sb", [P, 2, 2])
        f2_rest = sb("f2_rest", [P, 2, 2])
        s2 = sb("s2", [P, 2, P + 3], BF16)
        t2_left = sb("t2_left", [P, N], BF16)
        t2_right = sb("t2_right", [P, 2, N], BF16)
        att2 = sb("att2", [P, 2, N])
        nm2 = sb("nm2", [P, 2])
        sm2 = sb("sm2", [P, 2])
        rc2 = sb("rc2", [P, 2])
        pt2_hi = sb("pt2_hi", [P, 2 * N], F32R)
        pt2_lo = sb("pt2_lo", [P, 2 * N], F32R)
        ov = sb("ov", [P, 2, F])
        oe = sb("oe", [P, 2, F])
        o_sb = sb("o_sb", [P, 2, F])
        ot_hi = sb("ot_hi", [P, C, 2 * N], F32R)
        ot_lo = sb("ot_lo", [P, C, 2 * N], F32R)
        d_sb = sb("d_sb", [P, C, 2 * N])
        d_hi = sb("d_hi", [P, C, 2 * N], F32R)
        d_lo = sb("d_lo", [P, C, 2 * N], F32R)
        r_sb = sb("r_sb", [P, 2, F])
        out_sb = sb("out_sb", [P, 2, 2, F])
        bn0, bn1, bn2 = (sb(f"bn{i}", [P, 2, 6]) for i in range(3))
        mv0, mv1, mv2 = (sb(f"mv{i}", [P, 2, 2]) for i in range(3))
        ve0, ve1, ve2 = (sb(f"ve{i}", [P, 2]) for i in range(3))
        eps_col = sb("eps_col", [P, 2])
        zeros = sb("zeros", [P, 2, 2, H])
        half_col = sb("half_col", [P, 2])
        rs0, rs1, rs2 = (sb(f"rs{i}", [P, 2]) for i in range(3))
        a_all = x1b[:, :, :, :].rearrange("p a b f -> p a (b f)")
        ao_all = r_sb[:, :, :]
        b0_all = out_sb[:, 0, 0, :]
        adj_i = out_sb[:, 0, 1, 0:N].bitcast(I32)
        adjt_i = out_sb[:, 0, 1, N:2 * N].bitcast(I32)
        adj_f = out_sb[:, 1, 0, 0:N]
        ad_f = out_sb[:, 1, 1, :]
        junk = v0[:, 0, :]

        bank = [ctx.enter_context(nc.psum_tensor(f"bank{i}", [P, 512], F32)) for i in range(8)]
        S2_BANK = 4
        AX_BANK = (6, 4)
        Z2_BANK = 7
        G_BANK = (3, 0)
        B_BANK = 7
        PT2_BANK = 0
        PT_BANK = (5, 2)
        O_BANK = 1
        E_BANK = (5, 7, 3, 2)
        C_BANK = 1
        TR_BANK = 5
        F_BANK = 1
        H_BANK = (3, 6, 0, 3)
        D1_BANK = 1
        S_BANK = 2
        Z_BANK = (5, 4)
        D2_BANK = 2

        sems = """
            w_in c_in w_hi w_lo wa0 wao mask_ones ident0 ident ad0 ad1 ad2 ad3 ad_done db
            x_hi x_lo x_db ax ax_hi ax_lo b v0 bn0 mv0 ve0 rs0 x1 x1_hi x1_lo x1b c x1t f f_sb
            s1a s1b s1c s1d s1 s1t t1 z l1 lm1 nm1 e1 rc1 pn pt pt_hi pt_lo
            y y_hi y_lo h h_e h_u h_v h_hi h_lo g g_hi g_lo f2
            s2a s2b s2c s2d s2 s2t t2 z2 l2 lm2 nm2 e2 rc2 pt2 pt2_hi pt2_lo o ov oe ou o_sb vb
            tr ot_hi ot_lo d1 relu d_hi d_lo d2 yv bn1 mv1 ve1 rs1 q r bn2 mv2 ve2 rs2 out
        """.split()
        S = {n: ctx.enter_context(nc.semaphore(f"{n}_s")) for n in sems}
        x_in_s = [ctx.enter_context(nc.semaphore(f"x_in{i}_s")) for i in range(4)]
        out_s = [ctx.enter_context(nc.semaphore(f"out{i}_s")) for i in range(4)]
        block = ctx.enter_context(nc.Block())

        def plain(r):
            return r.bitcast(F32)

        def x_arrived(eng, p):
            if p.there():
                eng.wait_ge(x_in_s[p.slot(4)], (p.turn + p.off // 4 + 1) * 16)

        @block.sync
        def _(sp):
            sp.dma_start(adj_i, adj).then_inc(S["c_in"], 16)
            sp.dma_start(adjt_i, adj_t).then_inc(S["c_in"], 16)
            sp.dma_start(b0_all, b0.partition_broadcast(P)).then_inc(S["c_in"], 16)
            sp.dma_start(b2_all[:, :], b2.partition_broadcast(P)).then_inc(S["c_in"], 16)
            sp.dma_start(gamma_all[:, :], gamma.partition_broadcast(P)).then_inc(S["c_in"], 16)
            sp.dma_start(beta_all[:, :], beta.partition_broadcast(P)).then_inc(S["c_in"], 16)
            sp.dma_start(b1_col[:, :], b1).then_inc(S["c_in"], 16)
            sp.dma_start(a_all, a_heads.partition_broadcast(P)).then_inc(S["c_in"], 16)
            sp.dma_start(ao_all, a_out.rearrange("(a f) -> a f", a=2).partition_broadcast(P)).then_inc(S["c_in"], 16)

            def load(p):
                after(sp, S["v0"], p.back(4))
                if p.there():
                    sp.dma_start(x_in[:, p.slot(4)], x_pairs[p.index()]).then_inc(x_in_s[p.slot(4)], 16)

            for t in range(3):
                load(Pair(0, t, PAIRS))
            sp.dma_start(stage[:, 0:2 * C], w0_t.rearrange("(c p) o -> p c o", p=P)).then_inc(S["w_in"], 16)
            sp.dma_start(stage[:, 2 * C:3 * C], w1.rearrange("(c p) o -> p c o", p=P)).then_inc(S["w_in"], 16)
            sp.dma_start(stage[:, 3 * C:4 * C], w2.rearrange("(c p) o -> p c o", p=P)).then_inc(S["w_in"], 16)
            sp.wait_ge(S["w_lo"], 1)
            sp.dma_start(stage[:, :], w_heads.rearrange("h (c p) o -> p (h c) o", p=P)).then_inc(S["w_in"], 16)
            sp.wait_ge(S["w_lo"], 2)
            sp.wait_ge(S["wa0"], 2 * HC)
            sp.dma_start(stage[:, :], w_out.rearrange("(c p) o -> p c o", p=P)).then_inc(S["w_in"], 16)

            def step(t):
                r = t.back(5)
                load(Pair(t.turn, t.off + 3, PAIRS))
                if r.there():
                    after(sp, S["out"], r, 2)
                    sp.dma_start(out_pairs[r.index()], out_sb[:, r.slot(2)]).then_inc(out_s[r.slot(4)], 16)

            over_steps(sp, PAIRS, step)
            for i in range(4):
                sp.wait_ge(out_s[i], 16 * (PAIRS // 4))

        @block.tensor
        def _(pe):
            def triple(ps, a_hi, a_lo, b_hi, b_lo, start, stop):
                nc.tensor.matmul(ps, a_hi, b_hi, start=start, stop=False)
                nc.tensor.matmul(ps, a_hi, b_lo, start=False, stop=False)
                return nc.tensor.matmul(ps, a_lo, b_hi, start=False, stop=stop)

            def ax_products(p, b):
                if not p.there():
                    return
                if b == 0:
                    after(pe, S["x_hi"], p)
                    after(pe, S["x_lo"], p)
                    if p.off == 0:
                        pe.wait_ge(S["ad_done"], 2)
                i = p.slot(2)
                for c in range(C):
                    last = triple(bank[AX_BANK[b]][:, c * 2 * N:(c + 1) * 2 * N],
                                  x_hi[:, i, b, c * P:(c + 1) * P], x_lo[:, i, b, c * P:(c + 1) * P],
                                  ad_hi[:, :], ad_lo[:, :], c == 0, c == C - 1)
                last.then_inc(S["ax"], 1)

            def y_products(m, u):
                if not m.there():
                    return
                b, c = u // C, u % C
                if c == 0:
                    after(pe, S["pt_hi"], m, 2, b + 1)
                    after(pe, S["pt_lo"], m, 2, b + 1)
                if u == 0:
                    after(pe, S["x1_hi"], m)
                    after(pe, S["x1_lo"], m)
                i = m.slot(2)
                triple(bank[E_BANK[u]][:, :], x1_hi[:, i, b, c * P:(c + 1) * P], x1_lo[:, i, b, c * P:(c + 1) * P],
                       pt_hi[:, b], pt_lo[:, b], True, True).then_inc(S["y"], 1)

            def s2_transposes(q):
                if not q.there():
                    return
                after(pe, S["s2"], q)
                ps = bank[S2_BANK][:, :].bitcast(BF16)
                for side in range(2):
                    last = nc.tensor.transpose(ps[:, side * N:(side + 1) * N],
                                               s2[:, :, :].rearrange("p s w -> p (s w)")[:, side * P:(side + 1) * P],
                                               identb[:, :])
                last.then_inc(S["s2t"], 1)

            def b_products(p, b):
                if not p.there():
                    return
                if p.off == 0 and b == 0:
                    pe.wait_ge(S["w_hi"], 1)
                    pe.wait_ge(S["w_lo"], 1)
                after(pe, S["ax_hi"], p, 2, b + 1)
                after(pe, S["ax_lo"], p, 2, b + 1)
                for k in range(2 * C):
                    side, c = k // C, k % C
                    cols = slice(N, 2 * N) if side == 0 else slice(0, N)
                    last = triple(bank[B_BANK][:, b * F:(b + 1) * F], ax_hi[:, b, c, cols], ax_lo[:, b, c, cols],
                                  w_hi[:, W0 + k], w_lo[:, W0 + k], k == 0, k == 2 * C - 1)
                last.then_inc(S["b"], 1)

            def z2_products(q):
                if not q.there():
                    return
                after(pe, S["t2"], q, 3)
                ps = bank[Z2_BANK]
                nc.tensor.matmul(ps[:, 0:2 * N], identb[:, :], mask[:, 0:2], start=True, stop=False)
                nc.tensor.matmul(ps[:, 0:2 * N], t2_left[:, :], t2_right[:, :, :], start=False, stop=True)\
                    .then_inc(S["z2"], 1)

            def g_products(g, b):
                if not g.there():
                    return
                if b == 0:
                    if g.off == 0:
                        pe.wait_ge(S["w_lo"], 3)
                        pe.wait_ge(S["w_hi"], 3)
                for k in range(HC):
                    if b == 0 and k % C == 0:
                        after(pe, S["h_hi"], g, H, k // C + 1)
                        after(pe, S["h_lo"], g, H, k // C + 1)
                    last = triple(bank[G_BANK[b]][:, 0:F + 2], h_hi[:, k, b], h_lo[:, k, b], wo_hi[:, k], wo_lo[:, k],
                                  k == 0, k == HC - 1)
                last.then_inc(S["g"], 1)

            def c_transposes(p):
                if not p.there():
                    return
                after(pe, S["x1"], p, 2)
                for b in range(2):
                    for c in range(C):
                        k = b * C + c
                        last = nc.tensor.transpose(bank[C_BANK][:, k * N:(k + 1) * N],
                                                   x1[:, p.slot(2), b, c * P:(c + 1) * P], ident[:, :])
                last.then_inc(S["c"], 1)

            def pt2_transposes(q):
                if not q.there():
                    return
                after(pe, S["e2"], q)
                for b in range(2):
                    last = nc.tensor.transpose(bank[PT2_BANK][:, b * N:(b + 1) * N], att2[:, b], ident[:, :])
                last.then_inc(S["pt2"], 1)

            def f_products(p):
                if not p.there():
                    return
                after(pe, S["x1t"], p)
                if p.off == 0:
                    pe.wait_ge(S["wa0"], 2 * HC)
                for b in range(2):
                    for c in range(C):
                        last = nc.tensor.matmul(bank[F_BANK][:, b * 2 * H:(b + 1) * 2 * H], x1t[:, b, c], wa[:, c],
                                                start=c == 0, stop=c == C - 1)
                last.then_inc(S["f"], 1)

            def o_products(q):
                if not q.there():
                    return
                after(pe, S["pt2_hi"], q)
                after(pe, S["pt2_lo"], q)
                for b in range(2):
                    last = triple(bank[O_BANK][:, b * F:(b + 1) * F], pt2_hi[:, b * N:(b + 1) * N],
                                  pt2_lo[:, b * N:(b + 1) * N], g_hi[:, q.slot(2), b], g_lo[:, q.slot(2), b], True, True)
                last.then_inc(S["o"], 1)

            def s_transposes(p):
                if not p.there():
                    return
                after(pe, S["s1"], p)
                ps = bank[S_BANK][:, :].bitcast(BF16)
                for b in range(2):
                    cols = s1[:, b].rearrange("p s w -> p (s w)")
                    for side in range(2):
                        k = 2 * b + side
                        last = nc.tensor.transpose(ps[:, k * N:(k + 1) * N], cols[:, side * P:(side + 1) * P],
                                                   identb[:, :])
                last.then_inc(S["s1t"], 1)

            def h_products(m, h):
                if not m.there():
                    return
                if h == 0:
                    after(pe, S["y_hi"], m, 4)
                    after(pe, S["y_lo"], m, 4)
                    if m.off == 0:
                        pe.wait_ge(S["w_hi"], 2)
                        pe.wait_ge(S["w_lo"], 2)
                for o in range(C):
                    for c in range(C):
                        k = WH + h * C + c
                        last = triple(bank[H_BANK[h]][:, o * 2 * N:(o + 1) * 2 * N], w_hi[:, k, o * P:(o + 1) * P],
                                      w_lo[:, k, o * P:(o + 1) * P], y_hi[:, c, h], y_lo[:, c, h],
                                      c == 0, c == C - 1)
                last.then_inc(S["h"], 1)

            def z_products(p, b):
                if not p.there():
                    return
                after(pe, S["t1"], p, H + 1)
                ps = bank[Z_BANK[b]]
                nc.tensor.matmul(ps[:, :], identb[:, :], mask[:, :, :], start=True, stop=False)
                nc.tensor.matmul(ps[:, :], t1_left[:, b], t1_right[:, b], start=False, stop=True)\
                    .then_inc(S["z"], 1)

            def o_transposes(q):
                if not q.there():
                    return
                after(pe, S["o_sb"], q)
                for b in range(2):
                    for c in range(C):
                        last = nc.tensor.transpose(bank[TR_BANK][:, (2 * c + b) * N:(2 * c + b + 1) * N],
                                                   o_sb[:, b, c * P:(c + 1) * P], ident[:, :])
                last.then_inc(S["tr"], 1)

            def d1_products(q):
                if not q.there():
                    return
                after(pe, S["ot_hi"], q)
                after(pe, S["ot_lo"], q)
                for d in range(C):
                    for c in range(C):
                        last = triple(bank[D1_BANK][:, d * 2 * N:(d + 1) * 2 * N], w_hi[:, W1 + c, d * P:(d + 1) * P],
                                      w_lo[:, W1 + c, d * P:(d + 1) * P], ot_hi[:, c], ot_lo[:, c],
                                      c == 0, c == C - 1)
                last.then_inc(S["d1"], 1)

            def d2_products(q):
                if not q.there():
                    return
                after(pe, S["d_hi"], q)
                after(pe, S["d_lo"], q)
                for b in range(2):
                    for c in range(C):
                        last = triple(bank[D2_BANK][:, b * F:(b + 1) * F], d_hi[:, c, b * N:(b + 1) * N],
                                      d_lo[:, c, b * N:(b + 1) * N], w_hi[:, W2 + c], w_lo[:, W2 + c],
                                      c == 0, c == C - 1)
                last.then_inc(S["d2"], 1)

            def pt_transposes(p, b):
                if not p.there():
                    return
                after(pe, S["pn"], p, 2, b + 1)
                for h in range(H):
                    last = nc.tensor.transpose(bank[PT_BANK[b]][:, h * N:(h + 1) * N], att[:, b, h], ident[:, :])
                last.then_inc(S["pt"], 1)

            def step(t):
                after(pe, S["h_v"], t.back(3), 4, 2)
                ax_products(t, 0)
                after(pe, S["lm2"], t.back(4))
                b_products(t.back(1), 0)
                after(pe, S["lm1"], t.back(2), 2)
                ax_products(t, 1)
                after(pe, S["h_v"], t.back(3), 4, 3)
                pt2_transposes(t.back(4))
                b_products(t.back(1), 1)
                pt_transposes(t.back(2), 0)
                o_products(t.back(4))
                pt_transposes(t.back(2), 1)
                after(pe, S["h_v"], t.back(3), 4)
                g_products(t.back(3), 0)
                y_products(t.back(2), 0)
                y_products(t.back(2), 1)
                after(pe, S["ov"], t.back(4))
                c_transposes(t.back(1))
                after(pe, S["f2"], t.back(3), 2, 1)
                y_products(t.back(2), 2)
                y_products(t.back(2), 3)
                f_products(t.back(1))
                after(pe, S["y_lo"], t.back(2), 4, 1)
                o_transposes(t.back(4))
                g_products(t.back(3), 1)
                after(pe, S["y_lo"], t.back(2), 4)
                s_transposes(t.back(1))
                d1_products(t.back(4))
                h_products(t.back(2), 0)
                h_products(t.back(2), 1)
                z_products(t.back(1), 0)
                after(pe, S["ax_lo"], t, 2)
                s2_transposes(t.back(3))
                h_products(t.back(2), 2)
                z2_products(t.back(3))
                z_products(t.back(1), 1)
                d2_products(t.back(4))
                after(pe, S["h_v"], t.back(2), 4, 1)
                h_products(t.back(2), 3)

            pe.wait_ge(S["ident"], 2)
            over_steps(pe, PAIRS, step)

        @block.scalar
        def _(act):
            def split_weights(lot, src, hi):
                nc.scalar.activation(hi, src, ACT.Copy).then_inc(S["w_hi"], 1)

            act.wait_ge(S["mask_ones"], 1)
            act.wait_ge(S["w_in"], 16 * 3)
            hi_w = w_hi[:, :, :]
            nc.scalar.activation(hi_w[:, 0:2 * C], stage[:, 0:2 * C], ACT.Copy)
            nc.scalar.activation(hi_w[:, W1:W1 + 2 * C], stage[:, 2 * C:4 * C], ACT.Copy).then_inc(S["w_hi"], 1)
            act.wait_ge(S["w_in"], 16 * 4)
            nc.scalar.activation(hi_w[:, WH:WH + HC], stage[:, :], ACT.Copy).then_inc(S["w_hi"], 1)
            act.wait_ge(S["w_in"], 16 * 5)
            nc.scalar.activation(wo_hi[:, :, 0:F], stage[:, :], ACT.Copy)
            act.wait_ge(S["wao"], 2 * HC)
            nc.scalar.activation(wo_hi[:, :, F:F + 2], wao[:, :, :], ACT.Copy).then_inc(S["w_hi"], 1)

            def x_high(p):
                if p.there():
                    x_arrived(act, p)
                    nc.scalar.activation(x_hi[:, p.slot(2)], x_in[:, p.slot(4)], ACT.Copy).then_inc(S["x_hi"], 1)

            def pt_high(m, b):
                if m.there():
                    after(act, S["pt"], m, 2, b + 1)
                    nc.scalar.activation(pt_hi[:, b], bank[PT_BANK[b]][:, :], ACT.Copy).then_inc(S["pt_hi"], 1)

            def elu_exp(m, h):
                if m.there():
                    after(act, S["h"], m, H, h + 1)
                    if h < 2:
                        after(act, S["h_v"], m.back(1), H, h + 3)
                    else:
                        after(act, S["h_v"], m, H, h - 1)
                    nc.scalar.activation(elu[:, h % 2].rearrange("p c n -> p (c n)"), bank[H_BANK[h]][:, :],
                                         ACT.Exp).then_inc(S["h_e"], 1)

            def elu_high(m, h):
                if m.there():
                    after(act, S["h_v"], m, H, h + 1)
                    nc.scalar.activation(h_hi[:, h * C:(h + 1) * C].rearrange("p c b n -> p c (b n)"), hv[:, h % 2],
                                         ACT.Copy).then_inc(S["h_hi"], 1)

            def ax_high(p, b):
                if p.there():
                    after(act, S["ax"], p, 2, b + 1)
                    nc.scalar.activation(ax_hi[:, b].rearrange("p c n -> p (c n)"), bank[AX_BANK[b]][:, :],
                                         ACT.Copy).then_inc(S["ax_hi"], 1)

            def y_high(m, u):
                if m.there():
                    b, c = u // C, u % C
                    after(act, S["y"], m, 4, u + 1)
                    nc.scalar.activation(y_hi[:, c, :, b], bank[E_BANK[u]][:, :].rearrange("p (h n) -> p h n", h=H),
                                         ACT.Copy).then_inc(S["y_hi"], 1)

            def t2_copy(q):
                if q.there():
                    after(act, S["s2t"], q)
                    ps = bank[S2_BANK][:, :].bitcast(BF16)
                    nc.scalar.activation(t2_left[:, :], ps[:, 0:N], ACT.Copy).then_inc(S["t2"], 1)
                    for b in range(2):
                        rows = slice(32 * b, 32 * b + 32)
                        nc.scalar.activation(t2_right[rows, b], ps[rows, N:2 * N], ACT.Copy).then_inc(S["t2"], 1)

            def x1_high(p):
                if p.there():
                    after(act, S["x1"], p, 2)
                    nc.scalar.activation(x1_hi[:, p.slot(2)], x1[:, p.slot(2)], ACT.Copy).then_inc(S["x1_hi"], 1)

            def leaky2(q):
                if q.there():
                    after(act, S["z2"], q)
                    nc.scalar.activation(att2[:, :, :].rearrange("p b n -> p (b n)"), bank[Z2_BANK][:, 0:2 * N],
                                         ACT.Copy, scale=SLOPE).then_inc(S["l2"], 1)

            def exp2(q):
                if q.there():
                    after(act, S["nm2"], q)
                    for b in range(2):
                        last = nc.scalar.activation(att2[:, b], att2[:, b], ACT.Exp, bias=nm2[:, b:b + 1],
                                                    accum_out=sm2[:, b:b + 1])
                    last.then_inc(S["e2"], 1)

            def g_high(g, b):
                if g.there():
                    after(act, S["g"], g, 2, b + 1)
                    nc.scalar.activation(g_hi[:, g.slot(2), b], bank[G_BANK[b]][:, 0:F], ACT.Copy).then_inc(S["g_hi"], 1)

            def x1t_copy(p):
                if p.there():
                    after(act, S["c"], p)
                    nc.scalar.activation(x1t[:, :, :, :].rearrange("p b c n -> p (b c n)"), bank[C_BANK][:, :],
                                         ACT.Copy).then_inc(S["x1t"], 1)

            def pt2_high(q):
                if q.there():
                    after(act, S["pt2"], q)
                    nc.scalar.activation(pt2_hi[:, :], bank[PT2_BANK][:, 0:2 * N], ACT.Copy).then_inc(S["pt2_hi"], 1)

            def o_values(q):
                if q.there():
                    after(act, S["o"], q)
                    after(act, S["rc2"], q)
                    for b in range(2):
                        last = nc.scalar.activation(ov[:, b], bank[O_BANK][:, b * F:(b + 1) * F], ACT.Copy,
                                                    scale=rc2[:, b:b + 1])
                    last.then_inc(S["ov"], 1)

            def o_exp(q):
                if q.there():
                    after(act, S["ov"], q)
                    nc.scalar.activation(oe[:, :, :], ov[:, :, :], ACT.Exp).then_inc(S["oe"], 1)

            def t1_copy(p):
                if p.there():
                    after(act, S["s1t"], p)
                    ps = bank[S_BANK][:, :].bitcast(BF16)[:, 0:4 * N].rearrange("p (b s n) -> p b s n", b=2, s=2)
                    nc.scalar.activation(t1_left[:, :, :], ps[:, :, 0], ACT.Copy).then_inc(S["t1"], 1)
                    for h in range(H):
                        rows = slice(32 * h, 32 * h + 32)
                        nc.scalar.activation(t1_right[rows, :, h], ps[rows, :, 1], ACT.Copy).then_inc(S["t1"], 1)

            def leaky1(p, b):
                if p.there():
                    after(act, S["z"], p, 2, b + 1)
                    nc.scalar.activation(att[:, b].rearrange("p h n -> p (h n)"), bank[Z_BANK[b]][:, :], ACT.Copy,
                                         scale=SLOPE).then_inc(S["l1"], 1)

            def exp1(p, b):
                if p.there():
                    after(act, S["nm1"], p, 2, b + 1)
                    for h in range(H):
                        last = nc.scalar.activation(att[:, b, h], att[:, b, h], ACT.Exp, bias=nm1[:, b, h:h + 1],
                                                    accum_out=sm1[:, b, h:h + 1])
                    last.then_inc(S["e1"], 1)

            def ot_high(q):
                if q.there():
                    after(act, S["tr"], q)
                    nc.scalar.activation(ot_hi[:, :, :].rearrange("p c n -> p (c n)"), bank[TR_BANK][:, :],
                                         ACT.Copy).then_inc(S["ot_hi"], 1)

            def d_relu(q):
                if q.there():
                    after(act, S["d1"], q)
                    for d in range(C):
                        nc.scalar.activation(d_sb[:, d], bank[D1_BANK][:, d * 2 * N:(d + 1) * 2 * N], ACT.Relu,
                                             bias=b1_col[:, d:d + 1]).then_inc(S["relu"], 1)

            def d_high(q):
                if q.there():
                    after(act, S["relu"], q, 2)
                    nc.scalar.activation(d_hi[:, :, :], d_sb[:, :, :], ACT.Copy).then_inc(S["d_hi"], 1)

            def step(t):
                exp1(t.back(2), 0)
                exp2(t.back(4))
                exp1(t.back(2), 1)
                pt2_high(t.back(4))
                elu_exp(t.back(3), 3)
                elu_high(t.back(3), 2)
                x_high(Pair(t.turn, t.off + 1, PAIRS))
                after(act, S["b"], t.back(1), 2, 1)
                ax_high(t, 0)
                elu_high(t.back(3), 3)
                pt_high(t.back(2), 0)
                pt_high(t.back(2), 1)
                o_values(t.back(4))
                after(act, S["b"], t.back(1), 2)
                ax_high(t, 1)
                g_high(t.back(3), 0)
                o_exp(t.back(4))
                y_high(t.back(2), 0)
                y_high(t.back(2), 1)
                x1t_copy(t.back(1))
                y_high(t.back(2), 2)
                y_high(t.back(2), 3)
                x1_high(t.back(1))
                ot_high(t.back(4))
                g_high(t.back(3), 1)
                t1_copy(t.back(1))
                d_relu(t.back(4))
                elu_exp(t.back(2), 0)
                d_high(t.back(4))
                elu_exp(t.back(2), 1)
                leaky1(t.back(1), 0)
                t2_copy(t.back(3))
                elu_exp(t.back(2), 2)
                elu_high(t.back(2), 0)
                leaky2(t.back(3))
                elu_high(t.back(2), 1)
                leaky1(t.back(1), 1)

            x_high(Pair(0, 0, PAIRS))
            over_steps(act, PAIRS, step)

        @block.vector
        def _(dve):
            dve.wait_ge(S["c_in"], 16 * 9)
            nc.vector.tensor_copy(adj_f, adj_i)
            nc.vector.tensor_copy(ad_f[:, 0:N], adjt_i).then_inc(S["ad0"], 1)
            dve.wait_ge(S["ad0"], 1)
            nc.vector.reduce_sum(deg[:, :], adj_f, AX_X).then_inc(S["ad1"], 1)
            for h in range(H):
                nc.vector.tensor_scalar(mask[:, h], adj_f, 0.0, MASKED, ALU.is_le, ALU.mult)
            dve.wait_ge(S["ad1"], 1)
            dve.wait_ge(S["ident"], 2)
            nc.vector.tensor_scalar(ad_f[:, N:2 * N], ident[:, :], deg[:, 0:1], None, ALU.mult).then_inc(S["ad2"], 1)
            nc.vector.tensor_scalar(db[:, :], b0_all, deg[:, 0:1], None, ALU.mult).then_inc(S["db"], 1)
            dve.wait_ge(S["ad2"], 1)
            nc.vector.tensor_copy(ad_hi[:, :], ad_f).then_inc(S["ad3"], 1)
            dve.wait_ge(S["ad3"], 1)
            nc.vector.tensor_tensor(ad_lo[:, :], ad_f, plain(ad_hi[:, :]), ALU.subtract).then_inc(S["ad_done"], 2)

            dve.wait_ge(S["w_hi"], 1)
            nc.vector.tensor_tensor(w_lo[:, 0:2 * C], stage[:, 0:2 * C], plain(w_hi[:, 0:2 * C]), ALU.subtract)
            nc.vector.tensor_tensor(w_lo[:, W1:W1 + 2 * C], stage[:, 2 * C:4 * C], plain(w_hi[:, W1:W1 + 2 * C]),
                                    ALU.subtract).then_inc(S["w_lo"], 1)
            dve.wait_ge(S["w_hi"], 2)
            nc.vector.tensor_tensor(w_lo[:, WH:WH + HC], stage[:, :], plain(w_hi[:, WH:WH + HC]),
                                    ALU.subtract).then_inc(S["w_lo"], 1)
            done = 0
            for h in range(H):
                for c in range(C):
                    for side in range(2):
                        if done:
                            dve.wait_ge(S["wa0"], done)
                        nc.vector.tensor_tensor_reduce(junk, stage[:, h * C + c], a_all[:, h, side * F:(side + 1) * F],
                                                       1.0, 0.0, ALU.mult, ALU.add,
                                                       wa[:, c, side * H + h:side * H + h + 1]).then_inc(S["wa0"], 1)
                        done += 1
            done = 0
            dve.wait_ge(S["w_in"], 16 * 5)
            for k in range(HC):
                for side in range(2):
                    dve.wait_ge(S["wao"], done) if done else dve.wait_ge(S["wa0"], 2 * HC)
                    nc.vector.tensor_tensor_reduce(junk, stage[:, k], ao_all[:, side], 1.0, 0.0, ALU.mult, ALU.add,
                                                   wao[:, k, side:side + 1]).then_inc(S["wao"], 1)
                    done += 1
            dve.wait_ge(S["w_hi"], 3)
            dve.wait_ge(S["wao"], 2 * HC)
            nc.vector.tensor_tensor(wo_lo[:, :, 0:F], stage[:, :], plain(wo_hi[:, :, 0:F]), ALU.subtract)
            nc.vector.tensor_tensor(wo_lo[:, :, F:F + 2], wao[:, :, :], plain(wo_hi[:, :, F:F + 2]),
                                    ALU.subtract).then_inc(S["w_lo"], 1)

            def pt_low(m, b):
                if m.there():
                    after(dve, S["pt_hi"], m, 2, b + 1)
                    nc.vector.tensor_tensor(pt_lo[:, b], bank[PT_BANK[b]][:, :], plain(pt_hi[:, b]),
                                            ALU.subtract).then_inc(S["pt_lo"], 1)

            def elu_values(m, h):
                if m.there():
                    i = h % 2
                    after(dve, S["h_e"], m, H, h + 1)
                    nc.vector.tensor_scalar(elu[:, i], elu[:, i], 1.0, -1.0, ALU.min, ALU.add).then_inc(S["h_u"], 1)
                    after(dve, S["h_u"], m, H, h + 1)
                    if h < 2:
                        after(dve, S["h_lo"], m.back(1), H, h + 3)
                    else:
                        after(dve, S["h_lo"], m, H, h - 1)
                    nc.vector.scalar_tensor_tensor(out=hv[:, i].rearrange("p c n -> p (c n)"), in0=bank[H_BANK[h]][:, :],
                                                   scalar=0.0, in1=elu[:, i].rearrange("p c n -> p (c n)"),
                                                   op0=ALU.max, op1=ALU.add).then_inc(S["h_v"], 1)

            def ax_low(p, b):
                if p.there():
                    after(dve, S["ax_hi"], p, 2, b + 1)
                    nc.vector.tensor_tensor(ax_lo[:, b].rearrange("p c n -> p (c n)"), bank[AX_BANK[b]][:, :],
                                            plain(ax_hi[:, b].rearrange("p c n -> p (c n)")),
                                            ALU.subtract).then_inc(S["ax_lo"], 1)

            def y_low(m, u):
                if m.there():
                    b, c = u // C, u % C
                    after(dve, S["y_hi"], m, 4, u + 1)
                    nc.vector.tensor_tensor(y_lo[:, c, :, b], bank[E_BANK[u]][:, :].rearrange("p (h n) -> p h n", h=H),
                                            plain(y_hi[:, c, :, b]), ALU.subtract).then_inc(S["y_lo"], 1)

            def statistics(src, bn, bn_s):
                for b in range(2):
                    last = nc.vector.bn_stats(bn[:, b], src[:, b])
                last.then_inc(bn_s, 1)

            def moments(t, bn, mv, bn_s, mv_s, between):
                after(dve, bn_s, t)
                between()
                if not t.there():
                    return
                for b in range(2):
                    last = nc.vector.bn_aggr(mv[:, b], bn[:, b])
                last.then_inc(mv_s, 1)

            def first_norm(p):
                if p.there():
                    i = p.slot(2)
                    after(dve, S["b"], p, 2)
                    after(dve, S["x_db"], p)
                    nc.vector.tensor_tensor(v0[:, :, :].rearrange("p b f -> p (b f)"), bank[B_BANK][:, :],
                                            x_in[:, p.slot(4)].rearrange("p b f -> p (b f)"),
                                            ALU.add).then_inc(S["v0"], 1)
                    after(dve, S["v0"], p)
                    statistics(v0, bn0, S["bn0"])

            def first_scaled(p):
                if p.there():
                    i = p.slot(2)
                    after(dve, S["rs0"], p)
                    for b in range(2):
                        nc.vector.tensor_scalar(x1[:, i, b], v0[:, b], mv0[:, b, 0:1], rs0[:, b:b + 1],
                                                ALU.subtract, ALU.mult).then_inc(S["x1"], 1)

            def max2(q):
                if q.there():
                    after(dve, S["l2"], q)
                    flat = att2[:, :, :].rearrange("p b n -> p (b n)")
                    nc.vector.tensor_tensor(flat, bank[Z2_BANK][:, 0:2 * N], flat, ALU.max).then_inc(S["lm2"], 1)
                    after(dve, S["lm2"], q)
                    nc.vector.tensor_reduce(nm2[:, :], att2[:, :, :], AX_X, ALU.max, negate=True).then_inc(S["nm2"], 1)

            def g_low(g, b):
                if g.there():
                    after(dve, S["g_hi"], g, 2, b + 1)
                    i = g.slot(2)
                    nc.vector.tensor_tensor(g_lo[:, i, b], bank[G_BANK[b]][:, 0:F], plain(g_hi[:, i, b]),
                                            ALU.subtract).then_inc(S["g_lo"], 1)
                    if b == 0:
                        after(dve, S["s2"], g.back(1))
                    nc.vector.tensor_copy(f2_sb[:, b], bank[G_BANK[b]][:, F:F + 2]).then_inc(S["f2"], 1)

            def reciprocal2(q):
                if q.there():
                    after(dve, S["e2"], q)
                    nc.vector.reciprocal(rc2[:, :], sm2[:, :]).then_inc(S["rc2"], 1)

            def f_copy(p):
                if p.there():
                    after(dve, S["f"], p)
                    after(dve, S["s1"], p.back(1))
                    nc.vector.tensor_copy(f_sb[:, :, :, :].rearrange("p b s h -> p (b s h)"),
                                          bank[F_BANK][:, 0:4 * H]).then_inc(S["f_sb"], 1)

            def pt2_low(q):
                if q.there():
                    after(dve, S["pt2_hi"], q)
                    nc.vector.tensor_tensor(pt2_lo[:, :], bank[PT2_BANK][:, 0:2 * N], plain(pt2_hi[:, :]),
                                            ALU.subtract).then_inc(S["pt2_lo"], 1)

            def o_elu(q):
                if q.there():
                    after(dve, S["oe"], q)
                    nc.vector.tensor_scalar(oe[:, :, :], oe[:, :, :], 1.0, -1.0, ALU.min, ALU.add).then_inc(S["ou"], 1)
                    after(dve, S["ou"], q)
                    nc.vector.scalar_tensor_tensor(out=o_sb[:, :, :], in0=ov[:, :, :], scalar=0.0, in1=oe[:, :, :],
                                                   op0=ALU.max, op1=ALU.add).then_inc(S["o_sb"], 1)

            def max1(p, b):
                if p.there():
                    after(dve, S["l1"], p, 2, b + 1)
                    flat = att[:, b].rearrange("p h n -> p (h n)")
                    nc.vector.tensor_tensor(flat, bank[Z_BANK[b]][:, :], flat, ALU.max).then_inc(S["lm1"], 1)
                    after(dve, S["lm1"], p, 2, b + 1)
                    nc.vector.tensor_reduce(nm1[:, b], att[:, b], AX_X, ALU.max, negate=True).then_inc(S["nm1"], 1)

            def reciprocal1(p, b):
                if p.there():
                    after(dve, S["e1"], p, 2, b + 1)
                    nc.vector.reciprocal(rc1[:, b], sm1[:, b]).then_inc(S["rc1"], 1)

            def ot_low(q):
                if q.there():
                    after(dve, S["ot_hi"], q)
                    nc.vector.tensor_tensor(ot_lo[:, :, :].rearrange("p c n -> p (c n)"), bank[TR_BANK][:, :],
                                            plain(ot_hi[:, :, :].rearrange("p c n -> p (c n)")),
                                            ALU.subtract).then_inc(S["ot_lo"], 1)

            def norm_start(q):
                if not q.there():
                    return
                after(dve, S["d2"], q)
                after(dve, S["vb"], q)
                nc.vector.tensor_tensor(r_sb[:, :, :].rearrange("p b f -> p (b f)"), bank[D2_BANK][:, :],
                                        ov[:, :, :].rearrange("p b f -> p (b f)"), ALU.add).then_inc(S["yv"], 1)
                after(dve, S["yv"], q)
                statistics(r_sb, bn1, S["bn1"])

            def norm_scaled(q):
                if not q.there():
                    return
                after(dve, S["mv1"], q)
                for b in range(2):
                    last = nc.vector.scalar_tensor_tensor(out=r_sb[:, b], in0=r_sb[:, b], scalar=mv1[:, b, 0:1],
                                                          in1=gamma_all[:, :], op0=ALU.subtract, op1=ALU.mult)
                last.then_inc(S["q"], 1)
                after(dve, S["q"], q)
                after(dve, S["rs1"], q)
                for b in range(2):
                    last = nc.vector.scalar_tensor_tensor(out=r_sb[:, b], in0=r_sb[:, b], scalar=rs1[:, b:b + 1],
                                                          in1=x1b[:, q.slot(4), b], op0=ALU.mult, op1=ALU.add)
                last.then_inc(S["r"], 1)

            def last_statistics(q):
                if q.there():
                    after(dve, S["r"], q)
                    statistics(r_sb, bn2, S["bn2"])

            def norm_end(q):
                if not q.there():
                    return
                i = q.slot(2)
                after(dve, S["rs2"], q)
                before = q.back(2)
                if before.there():
                    dve.wait_ge(out_s[before.slot(4)], (before.turn + before.off // 4 + 1) * 16)
                for b in range(2):
                    nc.vector.tensor_scalar(out_sb[:, i, b], r_sb[:, b], mv2[:, b, 0:1], rs2[:, b:b + 1],
                                            ALU.subtract, ALU.mult).then_inc(S["out"], 1)

            def step(t):
                reciprocal1(t.back(2), 0)
                after(dve, S["out"], t.back(6), 2)
                norm_start(t.back(5))
                reciprocal1(t.back(2), 1)
                pt2_low(t.back(4))
                elu_values(t.back(3), 3)
                first_norm(t.back(1))
                moments(t.back(1), bn0, mv0, S["bn0"], S["mv0"],
                        lambda: reciprocal2(t.back(4)))
                pt_low(t.back(2), 0)
                pt_low(t.back(2), 1)
                first_scaled(t.back(1))
                moments(t.back(5), bn1, mv1, S["bn1"], S["mv1"],
                        lambda: g_low(t.back(3), 0))
                o_elu(t.back(4))
                y_low(t.back(2), 0)
                y_low(t.back(2), 1)
                y_low(t.back(2), 2)
                f_copy(t.back(1))
                ax_low(t, 0)
                y_low(t.back(2), 3)
                ot_low(t.back(4))
                norm_scaled(t.back(5))
                g_low(t.back(3), 1)
                last_statistics(t.back(5))
                moments(t.back(5), bn2, mv2, S["bn2"], S["mv2"],
                        lambda: ax_low(t, 1))
                elu_values(t.back(2), 0)
                norm_end(t.back(5))
                elu_values(t.back(2), 1)
                max1(t.back(1), 0)
                max2(t.back(3))
                max1(t.back(1), 1)
                elu_values(t.back(2), 2)

            over_steps(dve, PAIRS, step)

        @block.gpsimd
        def _(pool):
            for m in (ident, identb):
                nc.gpsimd.memset(m[:, :], 0.0).then_inc(S["ident0"], 1)
            pool.wait_ge(S["ident0"], 2)
            for m in (ident, identb):
                nc.gpsimd.affine_select(out=m[:, :], in_=m[:, :], compare_op=ALU.not_equal, fill=1.0, base=0,
                                        pattern=[[-1, P]], channel_multiplier=1).then_inc(S["ident"], 1)
            nc.gpsimd.memset(eps_col[:, :], EPS)
            nc.gpsimd.memset(half_col[:, :], -0.5)
            nc.gpsimd.memset(zeros[:, :, :, :], 0.0)
            nc.gpsimd.memset(t1_right[:, :, :, :], 0.0)
            nc.gpsimd.memset(t2_right[:, :, :], 0.0)
            nc.gpsimd.memset(s1[:, :, :, :], 0.0)
            nc.gpsimd.memset(s2[:, :, :], 0.0).then_inc(S["mask_ones"], 1)
            pool.wait_ge(S["mask_ones"], 1)
            s1_groups = s1[:, :, :, 0:P].rearrange("p b s (h w) -> p b s h w", h=H)
            s1_flat = s1[:, :, :, :].rearrange("p b s w -> p b (s w)")
            s2_groups = s2[:, :, 0:64].rearrange("p s (b w) -> p s b w", b=2)
            s2_flat = s2[:, :, :].rearrange("p s w -> p (s w)")
            for side, first in ((0, 3), (1, 0)):
                ones1 = s1_flat[:, :, side * P:(side + 1) * P].rearrange("p b (h w) -> p b h w", h=H)
                for b in range(2):
                    nc.gpsimd.memset(ones1[:, b, :, first:first + 3], 1.0)
                ones2 = s2_flat[:, side * P:side * P + 64].rearrange("p (b w) -> p b w", b=2)
                last = nc.gpsimd.memset(ones2[:, :, first:first + 3], 1.0)
            last.then_inc(S["mask_ones"], 1)
            pool.wait_ge(S["mask_ones"], 2)
            pool.wait_ge(S["db"], 1)

            def x_low(p):
                if p.there():
                    i, k = p.slot(2), p.slot(4)
                    after(pool, S["x_hi"], p)
                    nc.gpsimd.tensor_tensor(x_lo[:, i], x_in[:, k], plain(x_hi[:, i]), ALU.subtract)\
                        .then_inc(S["x_lo"], 1)

            def x_bias(p):
                if p.there():
                    k = p.slot(4)
                    after(pool, S["x_lo"], p)
                    nc.gpsimd.tensor_tensor(x_in[:, k], x_in[:, k], db[:, :].unsqueeze(1).to_broadcast([P, 2, F]),
                                            ALU.add).then_inc(S["x_db"], 1)

            def h_low(m, h):
                if m.there():
                    after(pool, S["h_hi"], m, H, h + 1)
                    hc = slice(h * C, (h + 1) * C)
                    nc.gpsimd.tensor_tensor(h_lo[:, hc].rearrange("p c b n -> p c (b n)"), hv[:, h % 2],
                                            plain(h_hi[:, hc]).rearrange("p c b n -> p c (b n)"),
                                            ALU.subtract).then_inc(S["h_lo"], 1)

            def x1_beta(p):
                if p.there():
                    after(pool, S["x1"], p, 2)
                    after(pool, S["r"], p.back(4))
                    nc.gpsimd.tensor_tensor(x1b[:, p.slot(4)], x1[:, p.slot(2)],
                                            beta_all[:, :].unsqueeze(1).to_broadcast([P, 2, F]),
                                            ALU.add).then_inc(S["x1b"], 1)

            def x1_low(p):
                if p.there():
                    i = p.slot(2)
                    after(pool, S["x1_hi"], p)
                    nc.gpsimd.tensor_tensor(x1_lo[:, i], x1[:, i], plain(x1_hi[:, i]), ALU.subtract)\
                        .then_inc(S["x1_lo"], 1)

            def three_parts(t, src, rest, zero, parts, sa, sb_, sc, sd, se):
                nc.gpsimd.tensor_tensor(parts(0), src, zero, ALU.add).then_inc(sa, 1)
                after(pool, sa, t)
                nc.gpsimd.tensor_tensor(rest, src, parts(0), ALU.subtract).then_inc(sb_, 1)
                after(pool, sb_, t)
                nc.gpsimd.tensor_tensor(parts(1), rest, zero, ALU.add).then_inc(sc, 1)
                after(pool, sc, t)
                nc.gpsimd.tensor_tensor(rest, rest, parts(1), ALU.subtract).then_inc(sd, 1)
                after(pool, sd, t)
                nc.gpsimd.tensor_tensor(parts(2), rest, zero, ALU.add).then_inc(se, 1)

            def s1_parts(p):
                if p.there():
                    after(pool, S["f_sb"], p)
                    after(pool, S["s1t"], p.back(1))
                    three_parts(p, f_sb[:, :, :, :], f_rest[:, :, :, :], zeros[:, :, :, :], lambda k: s1_groups[:, :, :, :, k],
                                S["s1a"], S["s1b"], S["s1c"], S["s1d"], S["s1"])

            def s2_parts(g):
                if g.there():
                    after(pool, S["f2"], g, 2)
                    after(pool, S["s2t"], g.back(1))
                    three_parts(g, f2_sb[:, :, :].rearrange("p b s -> p s b"),
                                f2_rest[:, :, :].rearrange("p b s -> p s b"), zeros[:, :, :, 0], lambda k: s2_groups[:, :, :, k],
                                S["s2a"], S["s2b"], S["s2c"], S["s2d"], S["s2"])

            def scales(t, mv, ve, rs, mv_s, ve_s, rs_s):
                if t.there():
                    after(pool, mv_s, t)
                    nc.gpsimd.tensor_tensor(ve[:, :], mv[:, :, 1], eps_col[:, :], ALU.add).then_inc(ve_s, 1)
                    after(pool, ve_s, t)
                    nc.gpsimd.tensor_tensor(rs[:, :], ve[:, :], half_col[:, :], ALU.pow).then_inc(rs_s, 1)

            def ffn_bias(q):
                if q.there():
                    after(pool, S["o_sb"], q)
                    nc.gpsimd.tensor_tensor(ov[:, :, :], o_sb[:, :, :],
                                            b2_all[:, :].unsqueeze(1).to_broadcast([P, 2, F]),
                                            ALU.add).then_inc(S["vb"], 1)

            def probabilities(p, b):
                if p.there():
                    after(pool, S["rc1"], p, 2, b + 1)
                    nc.gpsimd.tensor_tensor(att[:, b], att[:, b], rc1[:, b].unsqueeze(2).to_broadcast([P, H, N]),
                                            ALU.mult).then_inc(S["pn"], 1)

            def d_low(q):
                if q.there():
                    after(pool, S["d_hi"], q)
                    nc.gpsimd.tensor_tensor(d_lo[:, :, :], d_sb[:, :, :], plain(d_hi[:, :, :]),
                                            ALU.subtract).then_inc(S["d_lo"], 1)

            def step(t):
                x_bias(t.back(1))
                probabilities(t.back(2), 0)
                probabilities(t.back(2), 1)
                h_low(t.back(3), 2)
                h_low(t.back(3), 3)
                scales(t.back(1), mv0, ve0, rs0, S["mv0"], S["ve0"], S["rs0"])
                scales(t.back(5), mv1, ve1, rs1, S["mv1"], S["ve1"], S["rs1"])
                x_low(Pair(t.turn, t.off + 1, PAIRS))
                s1_parts(t.back(1))
                x1_low(t.back(1))
                s2_parts(t.back(3))
                scales(t.back(5), mv2, ve2, rs2, S["mv2"], S["ve2"], S["rs2"])
                d_low(t.back(4))
                ffn_bias(t.back(4))
                x1_beta(t.back(1))
                h_low(t.back(2), 0)
                h_low(t.back(2), 1)

            x_low(Pair(0, 0, PAIRS))
            over_steps(pool, PAIRS, step)


def kernel(x, adj, L0_gnn_W, L0_gnn_b, L1_gnn_W_heads, L1_gnn_a_heads, L1_gnn_W_out, L1_gnn_a_out, L1_gnn_w1,
           L1_gnn_b1, L1_gnn_w2, L1_gnn_b2, L1_gnn_ln_gamma, L1_gnn_ln_beta):
    import concourse.bacc as bacc
    import numpy as np
    from concourse.bass_utils import run_bass_kernel_spmd

    nc = bacc.Bacc("TRN2", target_bir_lowering=False, num_devices=1)
    laid_out = {
        "x": x, "adj": adj, "adj_t": np.asarray(adj).T, "w0_t": np.asarray(L0_gnn_W).T, "b0": L0_gnn_b,
        "w_heads": L1_gnn_W_heads, "a_heads": L1_gnn_a_heads, "w_out": L1_gnn_W_out, "a_out": L1_gnn_a_out,
        "w1": L1_gnn_w1, "b1": np.asarray(L1_gnn_b1).reshape(2, 128).T, "w2": L1_gnn_w2, "b2": L1_gnn_b2, "gamma": L1_gnn_ln_gamma,
        "beta": L1_gnn_ln_beta,
    }
    arrays, args = {}, []
    for name, a in laid_out.items():
        a = np.ascontiguousarray(a)
        arrays[f"in_{name}"] = a
        args.append(nc.dram_tensor(f"in_{name}", a.shape, mybir.dt.from_np(a.dtype), kind="ExternalInput").ap())
    args.append(nc.dram_tensor("out_x", arrays["in_x"].shape, F32, kind="ExternalOutput").ap())
    graph_layers(nc, *args)
    r = run_bass_kernel_spmd(nc, [arrays], core_ids=[0])
    return r.results[0]["out_x"]
```

```python
from contextlib import ExitStack

import concourse.bass as bass
from concourse import mybir

ALU = mybir.AluOpType
ACT = mybir.ActivationFunctionType
F32 = mybir.dt.float32
F32R = mybir.dt.float32r
BF16 = mybir.dt.bfloat16
I32 = mybir.dt.int32
AX_X = mybir.AxisListType.X

P = 128
UNROLL = 4
LAST_STAGE = 6
REACH = 8
AHEAD = 3
MASKED = -float(2**100)
EPS = 1e-5
SLOPE = 0.01


class Pair:

    def __init__(self, turn, off, pairs):
        self.turn, self.off, self.pairs = turn, off, pairs

    def back(self, k):
        return Pair(self.turn, self.off - k, self.pairs)

    def there(self):
        return not isinstance(self.turn, int) or 0 <= self.off < self.pairs

    def slot(self, n):
        return self.off % n

    def index(self):
        return self.turn * UNROLL + self.off

    def count(self, per, k):
        return self.turn * (UNROLL * per) + (self.off * per + k)


def after(eng, sem, pair, per=1, k=None):
    if pair.there():
        eng.wait_ge(sem, pair.count(per, per if k is None else k))


def over_steps(eng, pairs, step):
    full = (pairs - REACH - AHEAD) // UNROLL
    for t in range(REACH):
        step(Pair(0, t, pairs))
    with eng.Fori(0, full) as turn:
        for j in range(UNROLL):
            step(Pair(turn, REACH + j, pairs))
    for t in range(REACH + UNROLL * full, pairs + LAST_STAGE):
        step(Pair(0, t, pairs))


def graph_layers(nc, x, adj, adj_t, w0_t, b0, w_heads, w_heads_t, a_heads, w_out, w_out_t, a_out, w1, b1, w2, b2,
                 gamma, beta, out):
    graphs, N, F = x.shape
    H = w_heads.shape[0]
    C = F // P
    PAIRS = graphs // 2
    HC = H * C
    assert N == P and F == 2 * P and H == 4 and graphs % 2 == 0

    x_pairs = x.rearrange("(p b) n f -> p n b f", b=2)
    out_pairs = out.rearrange("(p b) n f -> p n b f", b=2)

    with ExitStack() as ctx:
        def sb(name, shape, dt=F32):
            return ctx.enter_context(nc.sbuf_tensor(name, shape, dt))

        W0, WH, W1, W2 = 0, 2 * C, 2 * C + HC, 3 * C + HC
        w_hi = sb("w_hi", [P, W2 + C, F], F32R)
        w_lo = sb("w_lo", [P, W2 + C, F], F32R)
        wo_hi = sb("wo_hi", [P, HC, F + 2], F32R)
        wo_lo = sb("wo_lo", [P, HC, F + 2], F32R)
        ad_hi = sb("ad_hi", [P, 2 * N], F32R)
        ad_lo = sb("ad_lo", [P, 2 * N], F32R)
        mask = sb("mask", [P, N])
        ident = sb("ident", [P, P])
        identb = sb("identb", [P, P], BF16)
        db = sb("db", [P, F])
        b2_all = sb("b2_all", [P, F])
        gamma_all = sb("gamma_all", [P, F])
        beta_all = sb("beta_all", [P, F])
        b1_col = sb("b1_col", [P, C])
        wa = sb("wa", [P, C, 2 * H])
        wao = sb("wao", [P, HC, 2])
        deg = sb("deg", [P, 1])
        heads_in = sb("heads_in", [P, HC, F])
        a_cols = sb("a_cols", [P, H, C, 2])
        ao_cols = sb("ao_cols", [P, C, 2])

        x_in = sb("x_in", [P, 4, 2, F])
        x_hi = sb("x_hi", [P, 2, 2, F], F32R)
        x_lo = sb("x_lo", [P, 2, 2, F], F32R)
        ax_hi = sb("ax_hi", [P, 2, C, 2 * N], F32R)
        ax_lo = sb("ax_lo", [P, 2, C, 2 * N], F32R)
        v0 = sb("v0", [P, 2, F])
        x1 = sb("x1", [P, 2, 2, F])
        x1_hi = sb("x1_hi", [P, 2, 2, F], F32R)
        x1_lo = sb("x1_lo", [P, 2, 2, F], F32R)
        x1b = sb("x1b", [P, 4, 2, F])
        x1t = sb("x1t", [P, 2, C, N])
        f_sb = sb("f_sb", [P, 2, 2, H])
        f_rest = sb("f_rest", [P, 2, 2, H])
        s1 = sb("s1", [P, 2, 2, P + 3], BF16)
        t1_left = sb("t1_left", [P, 2, N], BF16)
        t1_right = sb("t1_right", [P, 2, H, N], BF16)
        att = sb("att", [P, 2, H, N])
        nm1 = sb("nm1", [P, 2, H])
        sm1 = sb("sm1", [P, 2, H])
        rc1 = sb("rc1", [P, 2, H])
        pt_hi = sb("pt_hi", [P, 2, H * N], F32R)
        pt_lo = sb("pt_lo", [P, 2, H * N], F32R)
        y_hi = sb("y_hi", [P, C, H, 2, N], F32R)
        y_lo = sb("y_lo", [P, C, H, 2, N], F32R)
        elu = sb("elu", [P, 2, C, 2 * N])
        hv = sb("hv", [P, 2, C, 2 * N])
        h_hi = sb("h_hi", [P, HC, 2, N], F32R)
        h_lo = sb("h_lo", [P, HC, 2, N], F32R)
        g_hi = sb("g_hi", [P, 2, 2, F], F32R)
        g_lo = sb("g_lo", [P, 2, 2, F], F32R)
        f2_sb = sb("f2_sb", [P, 2, 2])
        f2_rest = sb("f2_rest", [P, 2, 2])
        s2 = sb("s2", [P, 2, P + 3], BF16)
        t2_left = sb("t2_left", [P, N], BF16)
        t2_right = sb("t2_right", [P, 2, N], BF16)
        att2 = sb("att2", [P, 2, N])
        nm2 = sb("nm2", [P, 2])
        sm2 = sb("sm2", [P, 2])
        rc2 = sb("rc2", [P, 2])
        pt2_hi = sb("pt2_hi", [P, 2 * N], F32R)
        pt2_lo = sb("pt2_lo", [P, 2 * N], F32R)
        ov = sb("ov", [P, 2, F])
        oe = sb("oe", [P, 2, F])
        o_sb = sb("o_sb", [P, 2, F])
        ot_hi = sb("ot_hi", [P, C, 2 * N], F32R)
        ot_lo = sb("ot_lo", [P, C, 2 * N], F32R)
        d_sb = sb("d_sb", [P, C, 2 * N])
        d_hi = sb("d_hi", [P, C, 2 * N], F32R)
        d_lo = sb("d_lo", [P, C, 2 * N], F32R)
        r_sb = sb("r_sb", [P, 2, F])
        out_sb = sb("out_sb", [P, 2, 2, F])
        bn0, bn1, bn2 = (sb(f"bn{i}", [P, 2, 6]) for i in range(3))
        mv0, mv1, mv2 = (sb(f"mv{i}", [P, 2, 2]) for i in range(3))
        ve0, ve1, ve2 = (sb(f"ve{i}", [P, 2]) for i in range(3))
        eps_col = sb("eps_col", [P, 2])
        zeros = sb("zeros", [P, 2, 2, H])
        half_col = sb("half_col", [P, 2])
        rs0, rs1, rs2 = (sb(f"rs{i}", [P, 2]) for i in range(3))
        b0_all = out_sb[:, 0, 0, :]
        adj_i = out_sb[:, 0, 1, 0:N].bitcast(I32)
        adjt_i = out_sb[:, 0, 1, N:2 * N].bitcast(I32)
        adj_f = out_sb[:, 1, 0, 0:N]
        ad_f = out_sb[:, 1, 1, :]
        w0_in = hv[:, :, :, :].rearrange("p i c n -> p (i c) n")
        w12_in = elu[:, :, :, :].rearrange("p i c n -> p (i c) n")
        heads_t_in = x1b[:, :, :, :].rearrange("p i b f -> p (i b) f")
        wo_in = [part[:, :, :] for part in (ov, oe, o_sb, d_sb)]
        wo_t_in = [hv[:, :, :, :].rearrange("p i c n -> p (i c n)"),
                   out_sb[:, :, :, :].rearrange("p i b f -> p (i b f)")]

        bank = [ctx.enter_context(nc.psum_tensor(f"bank{i}", [P, 512], F32)) for i in range(8)]
        S2_BANK = 4
        AX_BANK = (7, 1)
        Z2_BANK = 6
        G_BANK = (6, 3)
        B_BANK = 2
        PT2_BANK = 0
        PT_BANK = (3, 4)
        O_BANK = 5
        E_BANK = (3, 0, 4, 5)
        C_BANK = 5
        TR_BANK = 2
        F_BANK = 6
        H_BANK = (6, 3, 7, 2)
        D1_BANK = 5
        S_BANK = 2
        Z_BANK = (7, 0)
        D2_BANK = 4
        FREE_BANK = min(set(range(8)) - {*AX_BANK, B_BANK, C_BANK})

        sems = """
            adj_in c_in w0_in w12_in heads_in heads_t_in wo_in wo_t_in w_hi w_lo wa_p wao_p wa wao
            s_ones ident0 ident ad0 ad1 ad2 ad3 ad_done db
            x_hi x_lo x_db ax ax_hi ax_lo b v0 bn0 mv0 ve0 rs0 x1 x1_hi x1_lo x1b c x1t f f_sb
            s1a s1b s1c s1d s1 s1t t1 z l1 lm1 mk1 nm1 e1 rc1 pn pt pt_hi pt_lo
            y y_hi y_lo h h_e h_u h_v h_hi h_lo g g_hi f2
            s2a s2b s2c s2d s2 s2t t2 z2 l2 lm2 mk2 nm2 e2 rc2 pt2 pt2_hi pt2_lo o ov oe ou o_sb vb
            tr ot_hi ot_lo d1 relu d_hi d_lo d2 yv bn1 mv1 ve1 rs1 q r bn2 mv2 ve2 rs2 out
        """.split()
        S = {n: ctx.enter_context(nc.semaphore(f"{n}_s")) for n in sems}
        x_in_s = [ctx.enter_context(nc.semaphore(f"x_in{i}_s")) for i in range(4)]
        out_s = [ctx.enter_context(nc.semaphore(f"out{i}_s")) for i in range(4)]
        block = ctx.enter_context(nc.Block())

        def plain(r):
            return r.bitcast(F32)

        def x_arrived(eng, p):
            if p.there():
                eng.wait_ge(x_in_s[p.slot(4)], (p.turn + p.off // 4 + 1) * 16)

        @block.sync
        def _(sp):
            sp.dma_start(adj_i, adj).then_inc(S["adj_in"], 16)
            sp.dma_start(adjt_i, adj_t).then_inc(S["adj_in"], 16)
            sp.dma_start(b0_all, b0.partition_broadcast(P)).then_inc(S["adj_in"], 16)

            def load(p):
                after(sp, S["v0"], p.back(4))
                if p.there():
                    sp.dma_start(x_in[:, p.slot(4)], x_pairs[p.index()]).then_inc(x_in_s[p.slot(4)], 16)

            load(Pair(0, 0, PAIRS))
            sp.dma_start(w0_in, w0_t.rearrange("(c p) o -> p c o", p=P)).then_inc(S["w0_in"], 16)
            load(Pair(0, 1, PAIRS))
            sp.dma_start(a_cols[:, :, :, :], a_heads).then_inc(S["c_in"], 16)
            sp.dma_start(ao_cols[:, :, :], a_out).then_inc(S["c_in"], 16)
            sp.dma_start(heads_t_in, w_heads_t.rearrange("h (c p) i -> p (h c) i", p=P)).then_inc(S["heads_t_in"], 16)
            sp.dma_start(b2_all[:, :], b2.partition_broadcast(P)).then_inc(S["c_in"], 16)
            sp.dma_start(gamma_all[:, :], gamma.partition_broadcast(P)).then_inc(S["c_in"], 16)
            sp.dma_start(beta_all[:, :], beta.partition_broadcast(P)).then_inc(S["c_in"], 16)
            sp.dma_start(b1_col[:, :], b1).then_inc(S["c_in"], 16)
            sp.wait_ge(S["w_lo"], 1)
            sp.wait_ge(S["ad_done"], 2)
            for c in range(C):
                sp.dma_start(wo_t_in[c], w_out_t[c * P:(c + 1) * P, :]).then_inc(S["wo_t_in"], 16)
            sp.dma_start(heads_in[:, :, :], w_heads.rearrange("h (c p) o -> p (h c) o", p=P))\
                .then_inc(S["heads_in"], 16)
            load(Pair(0, 2, PAIRS))
            sp.dma_start(w12_in[:, 0:C], w1.rearrange("(c p) o -> p c o", p=P)).then_inc(S["w12_in"], 16)
            sp.dma_start(w12_in[:, C:2 * C], w2.rearrange("(c p) o -> p c o", p=P)).then_inc(S["w12_in"], 16)
            for i in range(4):
                sp.dma_start(wo_in[i], w_out[i * C * P:(i + 1) * C * P, :].rearrange("(c p) o -> p c o", p=P))\
                    .then_inc(S["wo_in"], 16)

            def step(t):
                r = t.back(6)
                load(Pair(t.turn, t.off + 3, PAIRS))
                if r.there():
                    after(sp, S["out"], r, 2)
                    sp.dma_start(out_pairs[r.index()], out_sb[:, r.slot(2)]).then_inc(out_s[r.slot(4)], 16)

            over_steps(sp, PAIRS, step)
            for i in range(4):
                sp.wait_ge(out_s[i], 16 * (PAIRS // 4))

        @block.tensor
        def _(pe):
            def triple(ps, a_hi, a_lo, b_hi, b_lo, start, stop):
                nc.tensor.matmul(ps, a_hi, b_hi, start=start, stop=False)
                nc.tensor.matmul(ps, a_hi, b_lo, start=False, stop=False)
                return nc.tensor.matmul(ps, a_lo, b_hi, start=False, stop=stop)

            def ax_products(p, b):
                if not p.there():
                    return
                if b == 0:
                    after(pe, S["x_hi"], p)
                    after(pe, S["x_lo"], p)
                    if p.off == 0:
                        pe.wait_ge(S["ad_done"], 2)
                i = p.slot(2)
                for c in range(C):
                    last = triple(bank[AX_BANK[b]][:, c * 2 * N:(c + 1) * 2 * N],
                                  x_hi[:, i, b, c * P:(c + 1) * P], x_lo[:, i, b, c * P:(c + 1) * P],
                                  ad_hi[:, :], ad_lo[:, :], c == 0, c == C - 1)
                last.then_inc(S["ax"], 1)

            def y_products(m, u):
                if not m.there():
                    return
                b, c = u // C, u % C
                if c == 0:
                    after(pe, S["pt_hi"], m, 2, b + 1)
                    after(pe, S["pt_lo"], m, 2, b + 1)
                if u == 0:
                    after(pe, S["x1_hi"], m)
                    after(pe, S["x1_lo"], m)
                i = m.slot(2)
                triple(bank[E_BANK[u]][:, :], x1_hi[:, i, b, c * P:(c + 1) * P], x1_lo[:, i, b, c * P:(c + 1) * P],
                       pt_hi[:, b], pt_lo[:, b], True, True).then_inc(S["y"], 1)

            def s2_transposes(q):
                if not q.there():
                    return
                after(pe, S["s2"], q)
                ps = bank[S2_BANK][:, :].bitcast(BF16)
                for side in range(2):
                    last = nc.tensor.transpose(ps[:, side * N:(side + 1) * N],
                                               s2[:, :, :].rearrange("p s w -> p (s w)")[:, side * P:(side + 1) * P],
                                               identb[:, :])
                last.then_inc(S["s2t"], 1)

            def b_products(p, b):
                if not p.there():
                    return
                if p.off == 0 and b == 0:
                    pe.wait_ge(S["w_hi"], 1)
                    pe.wait_ge(S["w_lo"], 1)
                after(pe, S["ax_hi"], p, 2, b + 1)
                after(pe, S["ax_lo"], p, 2, b + 1)
                for k in range(2 * C):
                    side, c = k // C, k % C
                    cols = slice(N, 2 * N) if side == 0 else slice(0, N)
                    last = triple(bank[B_BANK][:, b * F:(b + 1) * F], ax_hi[:, b, c, cols], ax_lo[:, b, c, cols],
                                  w_hi[:, W0 + k], w_lo[:, W0 + k], k == 0, k == 2 * C - 1)
                last.then_inc(S["b"], 1)

            def z2_products(q):
                if not q.there():
                    return
                after(pe, S["t2"], q, 3)
                ps = bank[Z2_BANK]
                nc.tensor.matmul(ps[:, 0:2 * N], t2_left[:, :], t2_right[:, :, :], start=True, stop=True)\
                    .then_inc(S["z2"], 1)

            def g_products(g, b):
                if not g.there():
                    return
                if b == 0:
                    if g.off == 0:
                        pe.wait_ge(S["w_lo"], 4)
                        pe.wait_ge(S["w_hi"], 4)
                for k in range(HC):
                    if b == 0 and k % C == 0:
                        after(pe, S["h_hi"], g, H, k // C + 1)
                        after(pe, S["h_lo"], g, H, k // C + 1)
                    last = triple(bank[G_BANK[b]][:, 0:F + 2], h_hi[:, k, b], h_lo[:, k, b], wo_hi[:, k], wo_lo[:, k],
                                  k == 0, k == HC - 1)
                last.then_inc(S["g"], 1)

            def head_vectors():
                ps = bank[FREE_BANK]
                pe.wait_ge(S["heads_t_in"], 16)
                pe.wait_ge(S["c_in"], 16 * 6)
                for i in range(C):
                    for h in range(H):
                        for c in range(C):
                            last = nc.tensor.matmul(ps[:, (i * H + h) * 2:(i * H + h + 1) * 2],
                                                    heads_t_in[:, h * C + c, i * P:(i + 1) * P], a_cols[:, h, c],
                                                    start=c == 0, stop=c == C - 1)
                last.then_inc(S["wa_p"], 1)

            def output_vector():
                ps = bank[S_BANK]
                pe.wait_ge(S["wo_t_in"], 16 * C)
                for k in range(HC):
                    for c in range(C):
                        last = nc.tensor.matmul(ps[:, 2 * k:2 * k + 2], wo_t_in[c][:, k * P:(k + 1) * P],
                                                ao_cols[:, c], start=c == 0, stop=c == C - 1)
                last.then_inc(S["wao_p"], 1)
                pe.wait_ge(S["wao"], 1)

            def c_transposes(p):
                if not p.there():
                    return
                if p.off == 0:
                    head_vectors()
                after(pe, S["x1"], p, 2)
                for b in range(2):
                    for c in range(C):
                        k = b * C + c
                        last = nc.tensor.transpose(bank[C_BANK][:, k * N:(k + 1) * N],
                                                   x1[:, p.slot(2), b, c * P:(c + 1) * P], ident[:, :])
                last.then_inc(S["c"], 1)

            def pt2_transposes(q):
                if not q.there():
                    return
                after(pe, S["e2"], q)
                for b in range(2):
                    last = nc.tensor.transpose(bank[PT2_BANK][:, b * N:(b + 1) * N], att2[:, b], ident[:, :])
                last.then_inc(S["pt2"], 1)

            def f_products(p):
                if not p.there():
                    return
                after(pe, S["x1t"], p)
                if p.off == 0:
                    pe.wait_ge(S["wa"], 1)
                for b in range(2):
                    for c in range(C):
                        last = nc.tensor.matmul(bank[F_BANK][:, b * 2 * H:(b + 1) * 2 * H], x1t[:, b, c], wa[:, c],
                                                start=c == 0, stop=c == C - 1)
                last.then_inc(S["f"], 1)

            def o_products(q):
                if not q.there():
                    return
                after(pe, S["pt2_hi"], q)
                after(pe, S["pt2_lo"], q)
                for b in range(2):
                    i = q.slot(2)
                    last = triple(bank[O_BANK][:, b * F:(b + 1) * F], pt2_hi[:, b * N:(b + 1) * N],
                                  pt2_lo[:, b * N:(b + 1) * N], g_hi[:, i, b], g_lo[:, i, b], True, True)
                last.then_inc(S["o"], 1)

            def s_transposes(p):
                if not p.there():
                    return
                if p.off == 0:
                    output_vector()
                after(pe, S["s1"], p)
                ps = bank[S_BANK][:, :].bitcast(BF16)
                for b in range(2):
                    cols = s1[:, b].rearrange("p s w -> p (s w)")
                    for side in range(2):
                        k = 2 * b + side
                        last = nc.tensor.transpose(ps[:, k * N:(k + 1) * N], cols[:, side * P:(side + 1) * P],
                                                   identb[:, :])
                last.then_inc(S["s1t"], 1)

            def h_products(m, h):
                if not m.there():
                    return
                if h == 0:
                    after(pe, S["y_hi"], m, 4)
                    after(pe, S["y_lo"], m, 4)
                    if m.off == 0:
                        pe.wait_ge(S["w_hi"], 2)
                        pe.wait_ge(S["w_lo"], 2)
                for o in range(C):
                    for c in range(C):
                        k = WH + h * C + c
                        last = triple(bank[H_BANK[h]][:, o * 2 * N:(o + 1) * 2 * N], w_hi[:, k, o * P:(o + 1) * P],
                                      w_lo[:, k, o * P:(o + 1) * P], y_hi[:, c, h], y_lo[:, c, h],
                                      c == 0, c == C - 1)
                last.then_inc(S["h"], 1)

            def z_products(p, b):
                if not p.there():
                    return
                after(pe, S["t1"], p, H + 1)
                ps = bank[Z_BANK[b]]
                nc.tensor.matmul(ps[:, :], t1_left[:, b], t1_right[:, b], start=True, stop=True)\
                    .then_inc(S["z"], 1)

            def o_transposes(q):
                if not q.there():
                    return
                after(pe, S["o_sb"], q)
                for b in range(2):
                    for c in range(C):
                        last = nc.tensor.transpose(bank[TR_BANK][:, (2 * c + b) * N:(2 * c + b + 1) * N],
                                                   o_sb[:, b, c * P:(c + 1) * P], ident[:, :])
                last.then_inc(S["tr"], 1)

            def d1_products(q):
                if not q.there():
                    return
                after(pe, S["ot_hi"], q)
                after(pe, S["ot_lo"], q)
                if q.off == 0:
                    pe.wait_ge(S["w_hi"], 3)
                    pe.wait_ge(S["w_lo"], 3)
                for d in range(C):
                    for c in range(C):
                        last = triple(bank[D1_BANK][:, d * 2 * N:(d + 1) * 2 * N], w_hi[:, W1 + c, d * P:(d + 1) * P],
                                      w_lo[:, W1 + c, d * P:(d + 1) * P], ot_hi[:, c], ot_lo[:, c],
                                      c == 0, c == C - 1)
                last.then_inc(S["d1"], 1)

            def d2_products(q):
                if not q.there():
                    return
                after(pe, S["d_hi"], q)
                after(pe, S["d_lo"], q)
                for b in range(2):
                    for c in range(C):
                        last = triple(bank[D2_BANK][:, b * F:(b + 1) * F], d_hi[:, c, b * N:(b + 1) * N],
                                      d_lo[:, c, b * N:(b + 1) * N], w_hi[:, W2 + c], w_lo[:, W2 + c],
                                      c == 0, c == C - 1)
                last.then_inc(S["d2"], 1)

            def pt_transposes(p, b):
                if not p.there():
                    return
                after(pe, S["pn"], p, 2, b + 1)
                for h in range(H):
                    last = nc.tensor.transpose(bank[PT_BANK[b]][:, h * N:(h + 1) * N], att[:, b, h], ident[:, :])
                last.then_inc(S["pt"], 1)

            def step(t):
                y_products(t.back(3), 1)
                y_products(t.back(3), 2)
                after(pe, S["f_sb"], t.back(2))
                g_products(t.back(4), 0)
                after(pe, S["ov"], t.back(5))
                y_products(t.back(3), 3)
                s_transposes(t.back(2))
                after(pe, S["y_lo"], t.back(3), 4, 1)
                g_products(t.back(4), 1)
                after(pe, S["ax_lo"], t.back(1), 2, 1)
                z_products(t.back(2), 0)
                o_transposes(t.back(5))
                after(pe, S["y_lo"], t.back(3), 4, 2)
                z_products(t.back(2), 1)
                h_products(t.back(3), 0)
                after(pe, S["f2"], t.back(4), 2)
                h_products(t.back(3), 1)
                s2_transposes(t.back(4))
                d1_products(t.back(5))
                b_products(t.back(1), 0)
                after(pe, S["h_v"], t.back(3), 4, 1)
                z2_products(t.back(4))
                b_products(t.back(1), 1)
                after(pe, S["lm1"], t.back(2), 2, 1)
                h_products(t.back(3), 2)
                after(pe, S["v0"], t.back(1))
                h_products(t.back(3), 3)
                d2_products(t.back(5))
                after(pe, S["h_v"], t.back(3), 4, 3)
                ax_products(t, 0)
                pt_transposes(t.back(2), 0)
                c_transposes(t.back(1))
                pt2_transposes(t.back(4))
                after(pe, S["yv"], t.back(5))
                pt_transposes(t.back(2), 1)
                ax_products(t, 1)
                f_products(t.back(1))
                y_products(t.back(2), 0)
                o_products(t.back(4))

            pe.wait_ge(S["ident"], 2)
            over_steps(pe, PAIRS, step)

        @block.scalar
        def _(act):
            def first_weights():
                act.wait_ge(S["w0_in"], 16)
                nc.scalar.activation(w_hi[:, W0:W0 + 2 * C], w0_in, ACT.Copy).then_inc(S["w_hi"], 1)

            def head_and_ffn_weights():
                act.wait_ge(S["heads_in"], 16)
                nc.scalar.activation(w_hi[:, WH:WH + HC], heads_in[:, :, :], ACT.Copy).then_inc(S["w_hi"], 1)
                act.wait_ge(S["w12_in"], 16 * 2)
                nc.scalar.activation(w_hi[:, W1:W1 + 2 * C], w12_in, ACT.Copy).then_inc(S["w_hi"], 1)
                act.wait_ge(S["w_lo"], 3)

            def output_weights():
                act.wait_ge(S["wo_in"], 16 * 4)
                for i in range(4):
                    nc.scalar.activation(wo_hi[:, i * C:(i + 1) * C, 0:F], wo_in[i], ACT.Copy)
                act.wait_ge(S["wao"], 1)
                nc.scalar.activation(wo_hi[:, :, F:F + 2], wao[:, :, :], ACT.Copy).then_inc(S["w_hi"], 1)
                act.wait_ge(S["w_lo"], 4)

            def x_high(p):
                if p.there():
                    x_arrived(act, p)
                    nc.scalar.activation(x_hi[:, p.slot(2)], x_in[:, p.slot(4)], ACT.Copy).then_inc(S["x_hi"], 1)

            def pt_high(m, b):
                if m.there():
                    after(act, S["pt"], m, 2, b + 1)
                    nc.scalar.activation(pt_hi[:, b], bank[PT_BANK[b]][:, :], ACT.Copy).then_inc(S["pt_hi"], 1)

            def elu_exp(m, h):
                if m.there():
                    if m.off == 0 and h == 0:
                        output_weights()
                    after(act, S["h"], m, H, h + 1)
                    if h < 2:
                        after(act, S["h_v"], m.back(1), H, h + 3)
                    else:
                        after(act, S["h_v"], m, H, h - 1)
                    nc.scalar.activation(elu[:, h % 2].rearrange("p c n -> p (c n)"), bank[H_BANK[h]][:, :],
                                         ACT.Exp).then_inc(S["h_e"], 1)

            def elu_high(m, h):
                if m.there():
                    after(act, S["h_v"], m, H, h + 1)
                    nc.scalar.activation(h_hi[:, h * C:(h + 1) * C].rearrange("p c b n -> p c (b n)"), hv[:, h % 2],
                                         ACT.Copy).then_inc(S["h_hi"], 1)

            def ax_high(p, b):
                if p.there():
                    after(act, S["ax"], p, 2, b + 1)
                    nc.scalar.activation(ax_hi[:, b].rearrange("p c n -> p (c n)"), bank[AX_BANK[b]][:, :],
                                         ACT.Copy).then_inc(S["ax_hi"], 1)

            def y_high(m, u):
                if m.there():
                    if m.off == 0 and u == 0:
                        head_and_ffn_weights()
                    b, c = u // C, u % C
                    after(act, S["y"], m, 4, u + 1)
                    nc.scalar.activation(y_hi[:, c, :, b], bank[E_BANK[u]][:, :].rearrange("p (h n) -> p h n", h=H),
                                         ACT.Copy).then_inc(S["y_hi"], 1)

            def t2_copy(q):
                if q.there():
                    after(act, S["s2t"], q)
                    ps = bank[S2_BANK][:, :].bitcast(BF16)
                    nc.scalar.activation(t2_left[:, :], ps[:, 0:N], ACT.Copy).then_inc(S["t2"], 1)
                    for b in range(2):
                        rows = slice(32 * b, 32 * b + 32)
                        nc.scalar.activation(t2_right[rows, b], ps[rows, N:2 * N], ACT.Copy).then_inc(S["t2"], 1)

            def x1_high(p):
                if p.there():
                    after(act, S["x1"], p, 2)
                    nc.scalar.activation(x1_hi[:, p.slot(2)], x1[:, p.slot(2)], ACT.Copy).then_inc(S["x1_hi"], 1)

            def leaky2(q):
                if q.there():
                    after(act, S["z2"], q)
                    nc.scalar.activation(att2[:, :, :].rearrange("p b n -> p (b n)"), bank[Z2_BANK][:, 0:2 * N],
                                         ACT.Copy, scale=SLOPE).then_inc(S["l2"], 1)

            def exp2(q):
                if q.there():
                    after(act, S["nm2"], q)
                    for b in range(2):
                        last = nc.scalar.activation(att2[:, b], att2[:, b], ACT.Exp, bias=nm2[:, b:b + 1],
                                                    accum_out=sm2[:, b:b + 1])
                    last.then_inc(S["e2"], 1)

            def g_high(g, b):
                if g.there():
                    after(act, S["g"], g, 2, b + 1)
                    nc.scalar.activation(g_hi[:, g.slot(2), b], bank[G_BANK[b]][:, 0:F], ACT.Copy)\
                        .then_inc(S["g_hi"], 1)

            def x1t_copy(p):
                if p.there():
                    after(act, S["c"], p)
                    nc.scalar.activation(x1t[:, :, :, :].rearrange("p b c n -> p (b c n)"), bank[C_BANK][:, :],
                                         ACT.Copy).then_inc(S["x1t"], 1)

            def pt2_high(q):
                if q.there():
                    after(act, S["pt2"], q)
                    nc.scalar.activation(pt2_hi[:, :], bank[PT2_BANK][:, 0:2 * N], ACT.Copy).then_inc(S["pt2_hi"], 1)

            def o_values(q):
                if q.there():
                    after(act, S["o"], q)
                    after(act, S["rc2"], q)
                    for b in range(2):
                        last = nc.scalar.activation(ov[:, b], bank[O_BANK][:, b * F:(b + 1) * F], ACT.Copy,
                                                    scale=rc2[:, b:b + 1])
                    last.then_inc(S["ov"], 1)

            def o_exp(q):
                if q.there():
                    after(act, S["ov"], q)
                    nc.scalar.activation(oe[:, :, :], ov[:, :, :], ACT.Exp).then_inc(S["oe"], 1)

            def t1_copy(p):
                if p.there():
                    after(act, S["s1t"], p)
                    ps = bank[S_BANK][:, :].bitcast(BF16)[:, 0:4 * N].rearrange("p (b s n) -> p b s n", b=2, s=2)
                    nc.scalar.activation(t1_left[:, :, :], ps[:, :, 0], ACT.Copy).then_inc(S["t1"], 1)
                    for h in range(H):
                        rows = slice(32 * h, 32 * h + 32)
                        nc.scalar.activation(t1_right[rows, :, h], ps[rows, :, 1], ACT.Copy).then_inc(S["t1"], 1)

            def leaky1(p, b):
                if p.there():
                    after(act, S["z"], p, 2, b + 1)
                    nc.scalar.activation(att[:, b].rearrange("p h n -> p (h n)"), bank[Z_BANK[b]][:, :], ACT.Copy,
                                         scale=SLOPE).then_inc(S["l1"], 1)

            def exp1(p, b):
                if p.there():
                    after(act, S["nm1"], p, 2, b + 1)
                    for h in range(H):
                        last = nc.scalar.activation(att[:, b, h], att[:, b, h], ACT.Exp, bias=nm1[:, b, h:h + 1],
                                                    accum_out=sm1[:, b, h:h + 1])
                    last.then_inc(S["e1"], 1)

            def ot_high(q):
                if q.there():
                    after(act, S["tr"], q)
                    nc.scalar.activation(ot_hi[:, :, :].rearrange("p c n -> p (c n)"), bank[TR_BANK][:, :],
                                         ACT.Copy).then_inc(S["ot_hi"], 1)

            def d_relu(q):
                if q.there():
                    after(act, S["d1"], q)
                    for d in range(C):
                        nc.scalar.activation(d_sb[:, d], bank[D1_BANK][:, d * 2 * N:(d + 1) * 2 * N], ACT.Relu,
                                             bias=b1_col[:, d:d + 1]).then_inc(S["relu"], 1)

            def d_high(q):
                if q.there():
                    after(act, S["relu"], q, 2)
                    nc.scalar.activation(d_hi[:, :, :], d_sb[:, :, :], ACT.Copy).then_inc(S["d_hi"], 1)

            def step(t):
                o_values(t.back(5))
                y_high(t.back(3), 1)
                y_high(t.back(3), 2)
                o_exp(t.back(5))
                g_high(t.back(4), 0)
                y_high(t.back(3), 3)
                t1_copy(t.back(2))
                ax_high(t.back(1), 1)
                g_high(t.back(4), 1)
                leaky1(t.back(2), 0)
                ot_high(t.back(5))
                leaky1(t.back(2), 1)
                x_high(Pair(t.turn, t.off + 1, PAIRS))
                elu_exp(t.back(3), 0)
                x1_high(t.back(2))
                elu_exp(t.back(3), 1)
                t2_copy(t.back(4))
                elu_high(t.back(3), 0)
                d_relu(t.back(5))
                elu_high(t.back(3), 1)
                d_high(t.back(5))
                leaky2(t.back(4))
                exp1(t.back(2), 0)
                elu_exp(t.back(3), 2)
                exp1(t.back(2), 1)
                elu_exp(t.back(3), 3)
                exp2(t.back(4))
                pt_high(t.back(2), 0)
                x1t_copy(t.back(1))
                pt2_high(t.back(4))
                pt_high(t.back(2), 1)
                elu_high(t.back(3), 2)
                ax_high(t, 0)
                y_high(t.back(2), 0)
                elu_high(t.back(3), 3)

            x_high(Pair(0, 0, PAIRS))
            first_weights()
            over_steps(act, PAIRS, step)

        @block.vector
        def _(dve):
            dve.wait_ge(S["adj_in"], 16 * 3)
            nc.vector.tensor_copy(adj_f, adj_i)
            nc.vector.tensor_copy(ad_f[:, 0:N], adjt_i).then_inc(S["ad0"], 1)
            dve.wait_ge(S["ad0"], 1)
            nc.vector.reduce_sum(deg[:, :], adj_f, AX_X).then_inc(S["ad1"], 1)
            nc.vector.tensor_scalar(mask[:, :], adj_f, 0.0, MASKED, ALU.is_le, ALU.mult)
            dve.wait_ge(S["ad1"], 1)
            dve.wait_ge(S["ident"], 2)
            nc.vector.tensor_scalar(ad_f[:, N:2 * N], ident[:, :], deg[:, 0:1], None, ALU.mult).then_inc(S["ad2"], 1)
            nc.vector.tensor_scalar(db[:, :], b0_all, deg[:, 0:1], None, ALU.mult).then_inc(S["db"], 1)
            dve.wait_ge(S["ad2"], 1)
            nc.vector.tensor_copy(ad_hi[:, :], ad_f).then_inc(S["ad3"], 1)
            dve.wait_ge(S["ad3"], 1)
            nc.vector.tensor_tensor(ad_lo[:, :], ad_f, plain(ad_hi[:, :]), ALU.subtract).then_inc(S["ad_done"], 2)

            def first_weights():
                dve.wait_ge(S["w_hi"], 1)
                nc.vector.tensor_tensor(w_lo[:, W0:W0 + 2 * C], w0_in, plain(w_hi[:, W0:W0 + 2 * C]),
                                        ALU.subtract).then_inc(S["w_lo"], 1)

            def head_and_ffn_weights():
                dve.wait_ge(S["w_hi"], 2)
                nc.vector.tensor_tensor(w_lo[:, WH:WH + HC], heads_in[:, :, :], plain(w_hi[:, WH:WH + HC]),
                                        ALU.subtract).then_inc(S["w_lo"], 1)
                dve.wait_ge(S["w_hi"], 3)
                nc.vector.tensor_tensor(w_lo[:, W1:W1 + 2 * C], w12_in, plain(w_hi[:, W1:W1 + 2 * C]),
                                        ALU.subtract).then_inc(S["w_lo"], 1)

            def output_weights():
                dve.wait_ge(S["w_hi"], 4)
                for i in range(4):
                    k = slice(i * C, (i + 1) * C)
                    nc.vector.tensor_tensor(wo_lo[:, k, 0:F], wo_in[i], plain(wo_hi[:, k, 0:F]), ALU.subtract)
                nc.vector.tensor_tensor(wo_lo[:, :, F:F + 2], wao[:, :, :], plain(wo_hi[:, :, F:F + 2]),
                                        ALU.subtract).then_inc(S["w_lo"], 1)

            def pt_low(m, b):
                if m.there():
                    after(dve, S["pt_hi"], m, 2, b + 1)
                    nc.vector.tensor_tensor(pt_lo[:, b], bank[PT_BANK[b]][:, :], plain(pt_hi[:, b]),
                                            ALU.subtract).then_inc(S["pt_lo"], 1)

            def elu_values(m, h):
                if m.there():
                    if m.off == 0 and h == 0:
                        output_weights()
                    i = h % 2
                    if m.off == 0 and h == 0:
                        dve.wait_ge(S["wao"], 1)
                    after(dve, S["h_e"], m, H, h + 1)
                    nc.vector.tensor_scalar(elu[:, i], elu[:, i], 1.0, -1.0, ALU.min, ALU.add).then_inc(S["h_u"], 1)
                    after(dve, S["h_u"], m, H, h + 1)
                    if h < 2:
                        after(dve, S["h_lo"], m.back(1), H, h + 3)
                    else:
                        after(dve, S["h_lo"], m, H, h - 1)
                    nc.vector.scalar_tensor_tensor(out=hv[:, i].rearrange("p c n -> p (c n)"),
                                                   in0=bank[H_BANK[h]][:, :],
                                                   scalar=0.0, in1=elu[:, i].rearrange("p c n -> p (c n)"),
                                                   op0=ALU.max, op1=ALU.add).then_inc(S["h_v"], 1)

            def ax_low(p, b):
                if p.there():
                    after(dve, S["ax_hi"], p, 2, b + 1)
                    nc.vector.tensor_tensor(ax_lo[:, b].rearrange("p c n -> p (c n)"), bank[AX_BANK[b]][:, :],
                                            plain(ax_hi[:, b].rearrange("p c n -> p (c n)")),
                                            ALU.subtract).then_inc(S["ax_lo"], 1)

            def y_low(m, u):
                if m.there():
                    if m.off == 0 and u == 0:
                        head_and_ffn_weights()
                    b, c = u // C, u % C
                    after(dve, S["y_hi"], m, 4, u + 1)
                    nc.vector.tensor_tensor(y_lo[:, c, :, b], bank[E_BANK[u]][:, :].rearrange("p (h n) -> p h n", h=H),
                                            plain(y_hi[:, c, :, b]), ALU.subtract).then_inc(S["y_lo"], 1)

            def statistics(src, bn, bn_s):
                for b in range(2):
                    last = nc.vector.bn_stats(bn[:, b], src[:, b])
                last.then_inc(bn_s, 1)

            def moments(t, bn, mv, bn_s, mv_s, between):
                after(dve, bn_s, t)
                between()
                if not t.there():
                    return
                for b in range(2):
                    last = nc.vector.bn_aggr(mv[:, b], bn[:, b])
                last.then_inc(mv_s, 1)

            def first_norm(p):
                if p.there():
                    after(dve, S["b"], p, 2)
                    after(dve, S["x_db"], p)
                    nc.vector.tensor_tensor(v0[:, :, :].rearrange("p b f -> p (b f)"), bank[B_BANK][:, :],
                                            x_in[:, p.slot(4)].rearrange("p b f -> p (b f)"),
                                            ALU.add).then_inc(S["v0"], 1)
                    after(dve, S["v0"], p)
                    statistics(v0, bn0, S["bn0"])

            def first_scaled(p):
                if p.there():
                    i = p.slot(2)
                    after(dve, S["rs0"], p)
                    for b in range(2):
                        nc.vector.tensor_scalar(x1[:, i, b], v0[:, b], mv0[:, b, 0:1], rs0[:, b:b + 1],
                                                ALU.subtract, ALU.mult).then_inc(S["x1"], 1)

            def max2(q):
                if q.there():
                    after(dve, S["l2"], q)
                    flat = att2[:, :, :].rearrange("p b n -> p (b n)")
                    nc.vector.tensor_tensor(flat, bank[Z2_BANK][:, 0:2 * N], flat, ALU.max).then_inc(S["lm2"], 1)

            def row_max2(q):
                if q.there():
                    after(dve, S["mk2"], q)
                    nc.vector.tensor_reduce(nm2[:, :], att2[:, :, :], AX_X, ALU.max, negate=True).then_inc(S["nm2"], 1)

            def g_low(g, b):
                if g.there():
                    after(dve, S["g_hi"], g, 2, b + 1)
                    i = g.slot(2)
                    nc.vector.tensor_tensor(g_lo[:, i, b], bank[G_BANK[b]][:, 0:F], plain(g_hi[:, i, b]),
                                            ALU.subtract)
                    if b == 0:
                        after(dve, S["s2"], g.back(1))
                    nc.vector.tensor_copy(f2_sb[:, b], bank[G_BANK[b]][:, F:F + 2]).then_inc(S["f2"], 1)

            def reciprocal2(q):
                if q.there():
                    after(dve, S["e2"], q)
                    nc.vector.reciprocal(rc2[:, :], sm2[:, :]).then_inc(S["rc2"], 1)

            def head_vectors():
                dve.wait_ge(S["wa_p"], 1)
                nc.vector.tensor_copy(wa[:, :, :].rearrange("p c (s h) -> p c h s", s=2),
                                      bank[FREE_BANK][:, 0:2 * HC].rearrange("p (c h s) -> p c h s", c=C, s=2))\
                    .then_inc(S["wa"], 1)

            def output_vector():
                dve.wait_ge(S["wao_p"], 1)
                nc.vector.tensor_copy(wao[:, :, :].rearrange("p k s -> p (k s)"), bank[S_BANK][:, 0:2 * HC])\
                    .then_inc(S["wao"], 1)

            def f_copy(p):
                if p.there():
                    if p.off == 0:
                        head_vectors()
                    after(dve, S["f"], p)
                    after(dve, S["s1"], p.back(1))
                    nc.vector.tensor_copy(f_sb[:, :, :, :].rearrange("p b s h -> p (b s h)"),
                                          bank[F_BANK][:, 0:4 * H]).then_inc(S["f_sb"], 1)
                    if p.off == 0:
                        output_vector()

            def pt2_low(q):
                if q.there():
                    after(dve, S["pt2_hi"], q)
                    nc.vector.tensor_tensor(pt2_lo[:, :], bank[PT2_BANK][:, 0:2 * N], plain(pt2_hi[:, :]),
                                            ALU.subtract).then_inc(S["pt2_lo"], 1)

            def o_elu(q):
                if q.there():
                    after(dve, S["oe"], q)
                    nc.vector.tensor_scalar(oe[:, :, :], oe[:, :, :], 1.0, -1.0, ALU.min, ALU.add).then_inc(S["ou"], 1)
                    after(dve, S["ou"], q)
                    nc.vector.scalar_tensor_tensor(out=o_sb[:, :, :], in0=ov[:, :, :], scalar=0.0, in1=oe[:, :, :],
                                                   op0=ALU.max, op1=ALU.add).then_inc(S["o_sb"], 1)

            def max1(p, b):
                if p.there():
                    after(dve, S["l1"], p, 2, b + 1)
                    flat = att[:, b].rearrange("p h n -> p (h n)")
                    nc.vector.tensor_tensor(flat, bank[Z_BANK[b]][:, :], flat, ALU.max).then_inc(S["lm1"], 1)

            def row_max1(p, b):
                if p.there():
                    after(dve, S["mk1"], p, 2, b + 1)
                    nc.vector.tensor_reduce(nm1[:, b], att[:, b], AX_X, ALU.max, negate=True).then_inc(S["nm1"], 1)

            def reciprocal1(p, b):
                if p.there():
                    after(dve, S["e1"], p, 2, b + 1)
                    nc.vector.reciprocal(rc1[:, b], sm1[:, b]).then_inc(S["rc1"], 1)

            def ot_low(q):
                if q.there():
                    after(dve, S["ot_hi"], q)
                    nc.vector.tensor_tensor(ot_lo[:, :, :].rearrange("p c n -> p (c n)"), bank[TR_BANK][:, :],
                                            plain(ot_hi[:, :, :].rearrange("p c n -> p (c n)")),
                                            ALU.subtract).then_inc(S["ot_lo"], 1)

            def norm_start(q):
                if not q.there():
                    return
                after(dve, S["d2"], q)
                after(dve, S["vb"], q)
                nc.vector.tensor_tensor(r_sb[:, :, :].rearrange("p b f -> p (b f)"), bank[D2_BANK][:, :],
                                        ov[:, :, :].rearrange("p b f -> p (b f)"), ALU.add).then_inc(S["yv"], 1)
                after(dve, S["yv"], q)
                statistics(r_sb, bn1, S["bn1"])

            def norm_scaled(q):
                if not q.there():
                    return
                after(dve, S["mv1"], q)
                for b in range(2):
                    last = nc.vector.scalar_tensor_tensor(out=r_sb[:, b], in0=r_sb[:, b], scalar=mv1[:, b, 0:1],
                                                          in1=gamma_all[:, :], op0=ALU.subtract, op1=ALU.mult)
                last.then_inc(S["q"], 1)
                after(dve, S["q"], q)
                after(dve, S["rs1"], q)
                after(dve, S["x1b"], q)
                for b in range(2):
                    last = nc.vector.scalar_tensor_tensor(out=r_sb[:, b], in0=r_sb[:, b], scalar=rs1[:, b:b + 1],
                                                          in1=x1b[:, q.slot(4), b], op0=ALU.mult, op1=ALU.add)
                last.then_inc(S["r"], 1)

            def last_statistics(q):
                if q.there():
                    after(dve, S["r"], q)
                    statistics(r_sb, bn2, S["bn2"])

            def norm_end(q):
                if not q.there():
                    return
                i = q.slot(2)
                after(dve, S["rs2"], q)
                before = q.back(2)
                if before.there():
                    dve.wait_ge(out_s[before.slot(4)], (before.turn + before.off // 4 + 1) * 16)
                for b in range(2):
                    nc.vector.tensor_scalar(out_sb[:, i, b], r_sb[:, b], mv2[:, b, 0:1], rs2[:, b:b + 1],
                                            ALU.subtract, ALU.mult).then_inc(S["out"], 1)

            def step(t):
                y_low(t.back(3), 0)
                norm_scaled(t.back(6))
                y_low(t.back(3), 1)
                o_elu(t.back(5))
                g_low(t.back(4), 0)
                y_low(t.back(3), 2)
                last_statistics(t.back(6))
                moments(t.back(6), bn2, mv2, S["bn2"], S["mv2"],
                        lambda: y_low(t.back(3), 3))
                ax_low(t.back(1), 1)
                g_low(t.back(4), 1)
                max1(t.back(2), 0)
                ot_low(t.back(5))
                max1(t.back(2), 1)
                elu_values(t.back(3), 0)
                elu_values(t.back(3), 1)
                row_max1(t.back(2), 0)
                row_max1(t.back(2), 1)
                norm_end(t.back(6))
                max2(t.back(4))
                first_norm(t.back(1))
                moments(t.back(1), bn0, mv0, S["bn0"], S["mv0"],
                        lambda: reciprocal1(t.back(2), 0))
                elu_values(t.back(3), 2)
                row_max2(t.back(4))
                reciprocal1(t.back(2), 1)
                first_scaled(t.back(1))
                after(dve, S["out"], t.back(6), 2)
                norm_start(t.back(5))
                moments(t.back(5), bn1, mv1, S["bn1"], S["mv1"],
                        lambda: pt_low(t.back(2), 0))
                pt2_low(t.back(4))
                pt_low(t.back(2), 1)
                elu_values(t.back(3), 3)
                f_copy(t.back(1))
                reciprocal2(t.back(4))
                ax_low(t, 0)

            first_weights()
            over_steps(dve, PAIRS, step)

        @block.gpsimd
        def _(pool):
            for m in (ident, identb):
                nc.gpsimd.memset(m[:, :], 0.0).then_inc(S["ident0"], 1)
            pool.wait_ge(S["ident0"], 2)
            for m in (ident, identb):
                nc.gpsimd.affine_select(out=m[:, :], in_=m[:, :], compare_op=ALU.not_equal, fill=1.0, base=0,
                                        pattern=[[-1, P]], channel_multiplier=1).then_inc(S["ident"], 1)
            nc.gpsimd.memset(eps_col[:, :], EPS)
            nc.gpsimd.memset(half_col[:, :], -0.5)
            nc.gpsimd.memset(zeros[:, :, :, :], 0.0)
            nc.gpsimd.memset(t1_right[:, :, :, :], 0.0)
            nc.gpsimd.memset(t2_right[:, :, :], 0.0)
            nc.gpsimd.memset(s1[:, :, :, :], 0.0)
            nc.gpsimd.memset(s2[:, :, :], 0.0).then_inc(S["s_ones"], 1)
            pool.wait_ge(S["s_ones"], 1)
            s1_groups = s1[:, :, :, 0:P].rearrange("p b s (h w) -> p b s h w", h=H)
            s1_flat = s1[:, :, :, :].rearrange("p b s w -> p b (s w)")
            s2_groups = s2[:, :, 0:64].rearrange("p s (b w) -> p s b w", b=2)
            s2_flat = s2[:, :, :].rearrange("p s w -> p (s w)")
            for side, first in ((0, 3), (1, 0)):
                ones1 = s1_flat[:, :, side * P:(side + 1) * P].rearrange("p b (h w) -> p b h w", h=H)
                for b in range(2):
                    nc.gpsimd.memset(ones1[:, b, :, first:first + 3], 1.0)
                ones2 = s2_flat[:, side * P:side * P + 64].rearrange("p (b w) -> p b w", b=2)
                last = nc.gpsimd.memset(ones2[:, :, first:first + 3], 1.0)
            last.then_inc(S["s_ones"], 1)
            pool.wait_ge(S["s_ones"], 2)
            pool.wait_ge(S["db"], 1)

            def x_low(p):
                if p.there():
                    i, k = p.slot(2), p.slot(4)
                    after(pool, S["x_hi"], p)
                    nc.gpsimd.tensor_tensor(x_lo[:, i], x_in[:, k], plain(x_hi[:, i]), ALU.subtract)\
                        .then_inc(S["x_lo"], 1)

            def x_bias(p):
                if p.there():
                    k = p.slot(4)
                    after(pool, S["x_lo"], p)
                    nc.gpsimd.tensor_tensor(x_in[:, k], x_in[:, k], db[:, :].unsqueeze(1).to_broadcast([P, 2, F]),
                                            ALU.add).then_inc(S["x_db"], 1)

            def h_low(m, h):
                if m.there():
                    after(pool, S["h_hi"], m, H, h + 1)
                    hc = slice(h * C, (h + 1) * C)
                    nc.gpsimd.tensor_tensor(h_lo[:, hc].rearrange("p c b n -> p c (b n)"), hv[:, h % 2],
                                            plain(h_hi[:, hc]).rearrange("p c b n -> p c (b n)"),
                                            ALU.subtract).then_inc(S["h_lo"], 1)

            def x1_beta(p):
                if p.there():
                    after(pool, S["x1"], p, 2)
                    if p.off == 0:
                        pool.wait_ge(S["c_in"], 16 * 6)
                        pool.wait_ge(S["wa"], 1)
                    after(pool, S["r"], p.back(4))
                    nc.gpsimd.tensor_tensor(x1b[:, p.slot(4)], x1[:, p.slot(2)],
                                            beta_all[:, :].unsqueeze(1).to_broadcast([P, 2, F]),
                                            ALU.add).then_inc(S["x1b"], 1)

            def x1_low(p):
                if p.there():
                    i = p.slot(2)
                    after(pool, S["x1_hi"], p)
                    nc.gpsimd.tensor_tensor(x1_lo[:, i], x1[:, i], plain(x1_hi[:, i]), ALU.subtract)\
                        .then_inc(S["x1_lo"], 1)

            def three_parts(t, src, rest, zero, parts, sa, sb_, sc, sd, se):
                nc.gpsimd.tensor_tensor(parts(0), src, zero, ALU.add).then_inc(sa, 1)
                after(pool, sa, t)
                nc.gpsimd.tensor_tensor(rest, src, parts(0), ALU.subtract).then_inc(sb_, 1)
                after(pool, sb_, t)
                nc.gpsimd.tensor_tensor(parts(1), rest, zero, ALU.add).then_inc(sc, 1)
                after(pool, sc, t)
                nc.gpsimd.tensor_tensor(rest, rest, parts(1), ALU.subtract).then_inc(sd, 1)
                after(pool, sd, t)
                nc.gpsimd.tensor_tensor(parts(2), rest, zero, ALU.add).then_inc(se, 1)

            def s1_parts(p):
                if p.there():
                    after(pool, S["f_sb"], p)
                    after(pool, S["s1t"], p.back(1))
                    three_parts(p, f_sb[:, :, :, :], f_rest[:, :, :, :], zeros[:, :, :, :],
                                lambda k: s1_groups[:, :, :, :, k],
                                S["s1a"], S["s1b"], S["s1c"], S["s1d"], S["s1"])

            def s2_parts(g):
                if g.there():
                    after(pool, S["f2"], g, 2)
                    after(pool, S["s2t"], g.back(1))
                    three_parts(g, f2_sb[:, :, :].rearrange("p b s -> p s b"),
                                f2_rest[:, :, :].rearrange("p b s -> p s b"), zeros[:, :, :, 0],
                                lambda k: s2_groups[:, :, :, k],
                                S["s2a"], S["s2b"], S["s2c"], S["s2d"], S["s2"])

            def scales(t, mv, ve, rs, mv_s, ve_s, rs_s):
                if t.there():
                    after(pool, mv_s, t)
                    nc.gpsimd.tensor_tensor(ve[:, :], mv[:, :, 1], eps_col[:, :], ALU.add).then_inc(ve_s, 1)
                    after(pool, ve_s, t)
                    nc.gpsimd.tensor_tensor(rs[:, :], ve[:, :], half_col[:, :], ALU.pow).then_inc(rs_s, 1)

            def ffn_bias(q):
                if q.there():
                    after(pool, S["o_sb"], q)
                    nc.gpsimd.tensor_tensor(ov[:, :, :], o_sb[:, :, :],
                                            b2_all[:, :].unsqueeze(1).to_broadcast([P, 2, F]),
                                            ALU.add).then_inc(S["vb"], 1)

            def mask1(p, b):
                if p.there():
                    after(pool, S["lm1"], p, 2, b + 1)
                    nc.gpsimd.tensor_tensor(att[:, b], att[:, b], mask[:, :].unsqueeze(1).to_broadcast([P, H, N]),
                                            ALU.add).then_inc(S["mk1"], 1)

            def mask2(q):
                if q.there():
                    after(pool, S["lm2"], q)
                    nc.gpsimd.tensor_tensor(att2[:, :, :], att2[:, :, :],
                                            mask[:, :].unsqueeze(1).to_broadcast([P, 2, N]),
                                            ALU.add).then_inc(S["mk2"], 1)

            def probabilities(p, b):
                if p.there():
                    after(pool, S["rc1"], p, 2, b + 1)
                    nc.gpsimd.tensor_tensor(att[:, b], att[:, b], rc1[:, b].unsqueeze(2).to_broadcast([P, H, N]),
                                            ALU.mult).then_inc(S["pn"], 1)

            def d_low(q):
                if q.there():
                    after(pool, S["d_hi"], q)
                    nc.gpsimd.tensor_tensor(d_lo[:, :, :], d_sb[:, :, :], plain(d_hi[:, :, :]),
                                            ALU.subtract).then_inc(S["d_lo"], 1)

            def step(t):
                h_low(t.back(4), 3)
                s1_parts(t.back(2))
                x1_beta(t.back(2))
                ffn_bias(t.back(5))
                x_bias(t.back(1))
                scales(t.back(6), mv2, ve2, rs2, S["mv2"], S["ve2"], S["rs2"])
                s2_parts(t.back(4))
                mask1(t.back(2), 0)
                mask1(t.back(2), 1)
                h_low(t.back(3), 0)
                x1_low(t.back(2))
                d_low(t.back(5))
                mask2(t.back(4))
                scales(t.back(1), mv0, ve0, rs0, S["mv0"], S["ve0"], S["rs0"])
                probabilities(t.back(2), 0)
                probabilities(t.back(2), 1)
                h_low(t.back(3), 1)
                x_low(Pair(t.turn, t.off + 1, PAIRS))
                scales(t.back(5), mv1, ve1, rs1, S["mv1"], S["ve1"], S["rs1"])
                h_low(t.back(3), 2)

            x_low(Pair(0, 0, PAIRS))
            over_steps(pool, PAIRS, step)


def kernel(x, adj, L0_gnn_W, L0_gnn_b, L1_gnn_W_heads, L1_gnn_a_heads, L1_gnn_W_out, L1_gnn_a_out, L1_gnn_w1,
           L1_gnn_b1, L1_gnn_w2, L1_gnn_b2, L1_gnn_ln_gamma, L1_gnn_ln_beta):
    import concourse.bacc as bacc
    import numpy as np
    from concourse.bass_utils import run_bass_kernel_spmd

    nc = bacc.Bacc("TRN2", target_bir_lowering=False, num_devices=1)
    laid_out = {
        "x": x, "adj": adj, "adj_t": np.asarray(adj).T, "w0_t": np.asarray(L0_gnn_W).T, "b0": L0_gnn_b,
        
        "w_heads": L1_gnn_W_heads, "w_heads_t": np.asarray(L1_gnn_W_heads).transpose(0, 2, 1),
        "a_heads": np.asarray(L1_gnn_a_heads).reshape(-1, 2, 2, 128).transpose(3, 0, 2, 1),
        "w_out": L1_gnn_W_out, "w_out_t": np.asarray(L1_gnn_W_out).T,
        "a_out": np.asarray(L1_gnn_a_out).reshape(2, 2, 128).transpose(2, 1, 0),
        "w1": L1_gnn_w1, "b1": np.asarray(L1_gnn_b1).reshape(2, 128).T, "w2": L1_gnn_w2, "b2": L1_gnn_b2,
        "gamma": L1_gnn_ln_gamma,
        "beta": L1_gnn_ln_beta,
    }
    arrays, args = {}, []
    for name, a in laid_out.items():
        a = np.ascontiguousarray(a)
        arrays[f"in_{name}"] = a
        args.append(nc.dram_tensor(f"in_{name}", a.shape, mybir.dt.from_np(a.dtype), kind="ExternalInput").ap())
    args.append(nc.dram_tensor("out_x", arrays["in_x"].shape, F32, kind="ExternalOutput").ap())
    graph_layers(nc, *args)
    r = run_bass_kernel_spmd(nc, [arrays], core_ids=[0])
    return r.results[0]["out_x"]
```
